# Optimizing a Trainium2 kernel written in Bass

```python
import numpy as np
import jax
import jax.numpy as jnp

def _softmax(x, axis=-1):
    return jax.nn.softmax(x, axis=axis)

def _gelu(x):
    return jax.nn.gelu(x, approximate=True)

def _silu(x):
    return jax.nn.silu(x)

def _sigmoid(x):
    return jax.nn.sigmoid(x)

def _layernorm(x, axis=-1, eps=1e-05):
    m = jnp.mean(x, axis=axis, keepdims=True)
    v = jnp.var(x, axis=axis, keepdims=True)
    return (x - m) / jnp.sqrt(v + eps)

def _scatter_add(tgt, idx, src, axis=0):
    return tgt.at[idx].add(src)

def _segment_sum(src, seg, n):
    return jax.ops.segment_sum(src, seg, n)
kernel_name = 'mk_xattn_ffn_d1_seqx_r8_dfa3d9'

def setup_inputs(seed: int=0):
    np.random.seed(seed)
    _w = jnp.asarray

    def _rec_inputs():
        import jax
        import jax.numpy as jnp
        _rk = jax.random.key(seed)
        x = -0.0002928 + 1 * jax.random.normal(jax.random.fold_in(_rk, 1), (8, 256, 128), jnp.float32)
        _lenS = 256 - jax.random.randint(jax.random.fold_in(_rk, 7), (8,), 0, max(1, 256 // 4) + 1, jnp.int32)
        _lenS2 = 256 - jax.random.randint(jax.random.fold_in(_rk, 8), (8,), 0, max(1, 256 // 4) + 1, jnp.int32)
        _ctx_1024P = jax.random.normal(jax.random.fold_in(_rk, 11), (8, 16, 128), jnp.float32)
        _ctx_1024c = jax.random.dirichlet(jax.random.fold_in(_rk, 511), 0.3 * jnp.ones((16,), jnp.float32), (8, 256))
        _ctx_1024t = jnp.einsum('bsk,bkd->bsd', _ctx_1024c, _ctx_1024P)
        _ctx_1024t = _ctx_1024t * jax.lax.rsqrt(jnp.mean(jnp.square(_ctx_1024t)) + 1e-12) * 0.953939
        ctx_1024 = -1.39393e-06 + 0.999914 * (_ctx_1024t + 0.3 * jax.random.normal(jax.random.fold_in(_rk, 611), (8, 256, 128), jnp.float32))
        _validS = jnp.arange(256)[None, :] < _lenS[:, None]
        _validS2 = jnp.arange(256)[None, :] < _lenS2[:, None]
        _causal = jnp.tril(jnp.ones((256, 256), dtype=bool))
        mask_BxSxS2_ik0 = jnp.where(jnp.broadcast_to(_validS2[:, None, :], (8, 256, 256)), 0, 1).astype(jnp.int32)
        return (x, ctx_1024, mask_BxSxS2_ik0)
    x, ctx_1024, mask_BxSxS2_ik0 = _rec_inputs()

    def _L0_xattn_setup():
        import jax, jax.numpy as jnp
        import numpy as np
        B, S, D, H = (2, 256, 128, 16)
        DK = D // H

        def _proj(x, w, b):
            y = jnp.einsum('bsd,ed->bse', x, w) + b
            return y.reshape(x.shape[0], -1, H, DK).transpose(0, 2, 1, 3)
        key = jax.random.key(seed)
        ks = jax.random.split(key, 12)
        scale = 1.0 / np.sqrt(D)
        inp = {'query': jax.random.normal(ks[0], (B, S, D), dtype=jnp.float32), 'key': jax.random.normal(ks[1], (B, S, D), dtype=jnp.float32), 'value': jax.random.normal(ks[2], (B, S, D), dtype=jnp.float32), 'mask': jnp.broadcast_to(jnp.tril(jnp.ones((S, S), dtype=jnp.int32)), (B, S, S)), 'wq': jax.random.normal(ks[3], (D, D), dtype=jnp.float32) * scale, 'bq': jnp.zeros((D,), dtype=jnp.float32), 'wk': jax.random.normal(ks[4], (D, D), dtype=jnp.float32) * scale, 'bk': jnp.zeros((D,), dtype=jnp.float32), 'wv': jax.random.normal(ks[5], (D, D), dtype=jnp.float32) * scale, 'bv': jnp.zeros((D,), dtype=jnp.float32), 'wo': jax.random.normal(ks[6], (D, D), dtype=jnp.float32) * scale, 'bo': jnp.zeros((D,), dtype=jnp.float32)}
        return inp
    _L0_xattn_all = _L0_xattn_setup()
    _L0_xattn_in = {k: v for k, v in _L0_xattn_all.items() if k in ('wq', 'bq', 'wk', 'bk', 'wv', 'bv', 'wo', 'bo')}
    del _L0_xattn_all

    def _L0_ffn_setup():
        import jax, jax.numpy as jnp
        import numpy as np
        B, T, C, E, H = (2, 256, 128, 4, 2730)
        key = jax.random.key(seed)
        ks = jax.random.split(key, 5)
        s = 0.02
        return {'x': jax.random.normal(ks[0], (B, T, C), dtype=jnp.float32), 'gate_w': jax.random.normal(ks[1], (E, C, H), dtype=jnp.float32) * s, 'gate_b': jnp.zeros((E, H), dtype=jnp.float32), 'up_w': jax.random.normal(ks[2], (E, C, H), dtype=jnp.float32) * s, 'up_b': jnp.zeros((E, H), dtype=jnp.float32), 'down_w': jax.random.normal(ks[3], (E, H, C), dtype=jnp.float32) * s, 'down_b': jnp.zeros((E, C), dtype=jnp.float32), 'router_w': jax.random.normal(ks[4], (C, E), dtype=jnp.float32) * s}
    _L0_ffn_all = _L0_ffn_setup()
    _L0_ffn_in = {k: v for k, v in _L0_ffn_all.items() if k in ('gate_w', 'gate_b', 'up_w', 'up_b', 'down_w', 'down_b', 'router_w')}
    del _L0_ffn_all
    return {'x': x, 'ctx_1024': ctx_1024, 'mask_BxSxS2_ik0': mask_BxSxS2_ik0, 'L0_xattn_wq': _L0_xattn_in['wq'], 'L0_xattn_bq': _L0_xattn_in['bq'], 'L0_xattn_wk': _L0_xattn_in['wk'], 'L0_xattn_bk': _L0_xattn_in['bk'], 'L0_xattn_wv': _L0_xattn_in['wv'], 'L0_xattn_bv': _L0_xattn_in['bv'], 'L0_xattn_wo': _L0_xattn_in['wo'], 'L0_xattn_bo': _L0_xattn_in['bo'], 'L0_ffn_gate_w': _L0_ffn_in['gate_w'], 'L0_ffn_gate_b': _L0_ffn_in['gate_b'], 'L0_ffn_up_w': _L0_ffn_in['up_w'], 'L0_ffn_up_b': _L0_ffn_in['up_b'], 'L0_ffn_down_w': _L0_ffn_in['down_w'], 'L0_ffn_down_b': _L0_ffn_in['down_b'], 'L0_ffn_router_w': _L0_ffn_in['router_w']}

def reference(x, ctx_1024, mask_BxSxS2_ik0, L0_xattn_wq, L0_xattn_bq, L0_xattn_wk, L0_xattn_bk, L0_xattn_wv, L0_xattn_bv, L0_xattn_wo, L0_xattn_bo, L0_ffn_gate_w, L0_ffn_gate_b, L0_ffn_up_w, L0_ffn_up_b, L0_ffn_down_w, L0_ffn_down_b, L0_ffn_router_w):
    import jax
    import jax.numpy as jnp

    def _L0_xattn_ref(query, key, value, mask, wq, bq, wk, bk, wv, bv, wo, bo):
        import jax, jax.numpy as jnp
        import numpy as np
        B, S, D, H = (2, 256, 128, 16)
        DK = D // H

        def _proj(x, w, b):
            y = jnp.einsum('bsd,ed->bse', x, w) + b
            return y.reshape(x.shape[0], -1, H, DK).transpose(0, 2, 1, 3)
        q = _proj(query, wq, bq)
        k = _proj(key, wk, bk)
        v = _proj(value, wv, bv)
        scores = jnp.einsum('bhqd,bhkd->bhqk', q, k) / jnp.sqrt(jnp.float32(DK))
        scores = jnp.where(mask[:, None, :, :] == 0, -jnp.inf, scores)
        p_attn = jax.nn.softmax(scores, axis=-1)
        x = jnp.einsum('bhqk,bhkd->bhqd', p_attn, v)
        x = x.transpose(0, 2, 1, 3).reshape(query.shape[0], -1, H * DK)
        return jnp.einsum('bsd,ed->bse', x, wo) + bo

    def _L0_ffn_ref(x, gate_w, gate_b, up_w, up_b, down_w, down_b, router_w):
        import jax, jax.numpy as jnp
        import numpy as np
        B, T, C, E, H = (2, 256, 128, 4, 2730)
        logits = jnp.einsum('btc,ce->bte', x, router_w)
        topk_vals, topk_idx = jax.lax.top_k(logits, 2)
        topk_weights = jax.nn.softmax(topk_vals, axis=-1)
        weights = jnp.sum(jax.nn.one_hot(topk_idx, E, dtype=x.dtype) * topk_weights[..., None], axis=-2)
        gate = jax.nn.silu(jnp.einsum('btc,ech->beth', x, gate_w) + gate_b[None, :, None, :])
        up = jnp.einsum('btc,ech->beth', x, up_w) + up_b[None, :, None, :]
        hidden = gate * up
        expert_out = jnp.einsum('beth,ehc->betc', hidden, down_w) + down_b[None, :, None, :]
        mixed = jnp.einsum('betc,bte->btc', expert_out, weights)
        return mixed
    x = x + _L0_xattn_ref(_layernorm(x, axis=-1), ctx_1024, ctx_1024, mask_BxSxS2_ik0, L0_xattn_wq, L0_xattn_bq, L0_xattn_wk, L0_xattn_bk, L0_xattn_wv, L0_xattn_bv, L0_xattn_wo, L0_xattn_bo)
    x = x + _L0_ffn_ref(_layernorm(x, axis=-1), L0_ffn_gate_w, L0_ffn_gate_b, L0_ffn_up_w, L0_ffn_up_b, L0_ffn_down_w, L0_ffn_down_b, L0_ffn_router_w)
    return x

_drawn_inputs = setup_inputs


def setup_inputs(seed=0):
    import zlib

    import numpy as np

    out = dict(_drawn_inputs(seed))
    spreads = {'L0_xattn_bq': (0.0, 0.287),
     'L0_xattn_bk': (0.0, 0.8),
     'L0_xattn_bv': (0.0, 0.1),
     'L0_xattn_bo': (0.0, 0.1),
     'L0_ffn_gate_b': (0.0, 0.8),
     'L0_ffn_up_b': (0.0, 0.8),
     'L0_ffn_down_b': (0.0, 0.1)}
    factors = {'L0_ffn_gate_w': 3.101, 'L0_ffn_up_w': 3.084, 'L0_ffn_down_w': 2.833}
    for name, (base, spread) in spreads.items():
        noise = np.random.default_rng([zlib.crc32(name.encode()), seed]).standard_normal(out[name].shape)
        drawn = base * np.exp(spread * noise) if base else spread * noise
        out[name] = jnp.asarray(drawn.astype(out[name].dtype))
    for name, factor in factors.items():
        out[name] = (out[name] * factor).astype(out[name].dtype)
    return out
```

```python
from contextlib import ExitStack

import concourse.bass as bass
from concourse import mybir
from concourse.alu_op_type import AluOpType as ALU

ACT = mybir.ActivationFunctionType
AX = mybir.AxisListType
F32, F32R, BF16, I32 = mybir.dt.float32, mybir.dt.float32r, mybir.dt.bfloat16, mybir.dt.int32

P = 128
B, S, D = 8, 256, 128
HEADS, DK = 16, 8
QT = S // P
G = 4
HG = HEADS // G
UNITS = QT * G
TOK = B * S
TILES = TOK // P
E, H = 4, 2730
FULL = H // P
TAIL = H - FULL * P
CH = FULL + 1
WRING = 3
TN = 512
TT = TOK // TN
STEPS = CH * TT
LAG = 2
UP0 = 64
SCALE = float(DK) ** -0.5
NEG = -1e30
LEAST = -3e38
EPS = 1e-5
C_ID, C_LOQ, C_LOK, C_HEAD, C_GE, C_GT, C_N = 0, P, P + 1, P + 2, P + 6, P + 22, P + 38
TASKS = [("TX", 1, 0), ("QK0", 2, 0), ("QK1", 3, 0), ("OVT1", 3, 1), ("QK2", 4, 0), ("OT", 4, 1),
         ("QK3", 5, 0), ("WO", 5, 1), ("V", 6, 0), ("OVT0", 7, 1)]
FRONT = ["TX", "QK0", "QK1", "QK2", "QK3", "V"]
BACK = ["OVT1", "OT", "WO"]


def tasks_of(first, last):
    return [t for t in TASKS if not (first and t[0] in BACK) and not (last and t[0] in FRONT)]


def tasks_before(b, first):
    return len(FRONT) if first else len(TASKS) * b + len(FRONT) + len(tasks_of(True, False)) - len(TASKS)


def need(engine, sem, value):
    if not isinstance(value, int) or value > 0:
        engine.wait_ge(sem, value)


def program(nc, x, ctxT, mask, wts, bqk, bv, bo, consts, wfull, wtail, dbT, router, wscratch, out):
    ctx = ExitStack()
    with ctx:
        def sb(name, shape, dt=F32):
            return ctx.enter_context(nc.sbuf_tensor(name, shape, dt))

        def sem(name):
            return ctx.enter_context(nc.semaphore(name))

        cst = sb("cst", [P, C_N])
        ident = cst[:, C_ID:C_ID + P]
        w4 = sb("w4", [P, 4, P])
        wqk = sb("wqk", [P, 2, G, 4, 32])
        bqk_sb = sb("bqk_sb", [P, 2, G])
        bv_sb = sb("bv_sb", [P, P])
        bo_sb = sb("bo_sb", [P, P])
        x1 = sb("x1", [P, TILES, P])
        stat = sb("stat", [P, TILES, 6])
        mv = sb("mv", [P, TILES, 2])
        rstd = sb("rstd", [P, TILES])
        expo = sb("expo", [P, TILES])
        one = sb("one", [P, 1])
        xn = sb("xn", [P, QT, P])
        xnT = sb("xnT", [P, S])
        ctx_sb = [sb(f"ctx{s}", [P, S]) for s in range(2)]
        mask_sb = [sb(f"mask{s}", [P, QT, S], I32) for s in range(2)]
        maskb = [sb(f"maskb{s}", [P, QT, S], BF16) for s in range(2)]
        mtop = [sb(f"mtop{s}", [P, QT]) for s in range(2)]
        nanfix = [sb(f"nanfix{s}", [P, QT]) for s in range(2)]
        qkf = [sb(f"qkf{r}", [P, 2, S]) for r in range(2)]
        qkhi = [sb(f"qkhi{r}", [P, 2, S], F32R) for r in range(2)]
        qkpack = [sb(f"qkpack{s}", [P, G, 2, S], F32R) for s in range(2)]
        qhead = [sb(f"qhead{s}", [P, G, HG, S], F32R) for s in range(2)]
        vaug = [sb(f"vaug{s}", [P, QT, HEADS, 32]) for s in range(2)]
        turn = sb("turn", [P, UNITS])
        top = [sb(f"top{r}", [P, HG]) for r in range(4)]
        negtop = [sb(f"negtop{r}", [P, HG]) for r in range(4)]
        masked = [sb(f"masked{r}", [P, HG, S]) for r in range(2)]
        prob = [sb(f"prob{r}", [P, HG, S]) for r in range(2)]
        probT = [sb(f"probT{r}", [P, HG, QT, P]) for r in range(2)]
        ov = sb("ov", [P, G, P])
        rden = sb("rden", [P, HEADS])
        onat = sb("onat", [P, QT, P])
        oT = sb("oT", [P, S])
        xn2 = sb("xn2", [P, TILES, P])
        acc = sb("acc", [P, TT, TN])
        rw = sb("rw", [P, E])
        lg = sb("lg", [P, TILES, E])
        cge = sb("cge", [P, TILES, E, E])
        cgt = sb("cgt", [P, TILES, E, E])
        rank = sb("rank", [P, TILES, E])
        ltop = sb("ltop", [P, TILES])
        wexp = sb("wexp", [P, TILES, E])
        wsum = sb("wsum", [P, TILES])
        mixw = sb("mixw", [P, E, TILES])
        mixwT = sb("mixwT", [E * TILES, P])
        mixb = sb("mixb", [P, E * TOK])
        db_sb = sb("db_sb", [P, E])
        wraw = [sb(f"wraw{r}", [P, 3 * P + 2]) for r in range(WRING)]
        whi = [sb(f"whi{r}", [P, 3 * P], F32R) for r in range(WRING)]
        wlo = [sb(f"wlo{r}", [P, 3 * P], F32R) for r in range(WRING)]
        wtraw = sb("wtraw", [P, 2 * P + 2])
        wbias = [sb(f"wbias{r}", [P, 2]) for r in range(WRING)]
        wtbias = sb("wtbias", [P, 2])
        wthi = sb("wthi", [P, 2 * P], F32R)
        wtlo = sb("wtlo", [P, 2 * P], F32R)
        xhalves = qhead[0][:, :, :, :].rearrange("p g h s -> p (g h s)")
        xhi, xlo = ([xhalves[:, (TT * half + t) * TN:(TT * half + t + 1) * TN] for t in range(TT)] for half in range(2))
        masked_flat = [v[:, :, :].rearrange("p h k -> p (h k)") for v in masked]
        xf = [masked_flat[t // 2][:, t % 2 * TN:(t % 2 + 1) * TN] for t in range(TT)]
        flat = [v[:, :, :].rearrange("p h k -> p (h k)") for v in prob] + \
               [v[:, :, :, :].rearrange("p h t q -> p (h t q)") for v in probT]
        gact, hid = ([f[:, n * TN:(n + 1) * TN] for n in range(2)] for f in flat[2:4])
        hhi = [sb(f"hhi{r}", [P, TN], F32R) for r in range(2)]
        hlo = [sb(f"hlo{r}", [P, TN], F32R) for r in range(2)]
        htail = [sb(f"htail{r}", [P, TN], F32R) for r in range(2)]
        mixed = [flat[t // 2][:, t % 2 * TN:(t % 2 + 1) * TN] for t in range(TT)]

        bank = [ctx.enter_context(nc.psum_tensor(f"bank{n}", [P, TN], F32)) for n in range(8)]
        scores = [[bank[0], bank[1]], [bank[2], bank[3]]]
        ptb, ovb, misc = [bank[4], bank[5]], bank[6], bank[7]

        s_cst, s_x, s_w4 = sem("cst_loaded"), sem("x_loaded"), sem("w4_loaded")
        s_ffnc = sem("ffn_consts_loaded")
        s_ctx = [sem(f"ctx_loaded{s}") for s in range(2)]
        s_mask = [sem(f"mask_loaded{s}") for s in range(2)]
        s_setup, s_psetup = sem("dve_setup_done"), sem("pool_setup_done")
        s_stat, s_var, s_rstd = sem("stats_made"), sem("variance_made"), sem("rstd_made")
        s_xb, s_xn = sem("bias_added"), sem("xn_made")
        s_mb, s_mtop, s_nan = sem("maskb_made"), sem("mask_top_made"), sem("nanfix_made")
        s_task, s_read = sem("task_done"), sem("task_read")
        s_qkf = sem("qk_copied")
        s_qkhi, s_pack, s_qh = sem("qk_high_rows_made"), sem("qk_packed"), sem("qhead_made")
        s_sc, s_top, s_nt = sem("scores_done"), sem("top_made"), sem("negtop_made")
        s_exp, s_pt = sem("probs_made"), sem("probs_transposed")
        s_pt0, s_pt1 = sem("half0_copied"), sem("half1_copied")
        s_pv, s_ov = sem("values_weighted"), sem("ov_copied")
        s_rden = sem("rden_made")
        s_stat2, s_var2 = sem("stats2_made"), sem("variance2_made")
        s_rstd2, s_xn2 = sem("rstd2_made"), sem("xn2_made")
        s_xt, s_x1t = sem("xn2_transposed"), sem("x1_transposed")
        s_xhi, s_xf, s_xlo = sem("xhi_made"), sem("xf_made"), sem("xlo_made")
        s_rt, s_top2, s_rexp = sem("routed"), sem("router_vector_step"), sem("router_exp")
        s_wT, s_wTc, s_wst, s_mixb = sem("mixw_transposed"), sem("mixwT_copied"), sem("mixw_stored"), sem("mixb_loaded")
        s_raw = [sem(f"wraw_loaded{r}") for r in range(WRING)]
        s_rawt = sem("wtail_loaded")
        s_wh, s_w = sem("weights_high_made"), sem("weights_split")
        s_gate, s_up, s_down = sem("gate_done"), sem("up_done"), sem("down_done")
        s_silu, s_h, s_hhi, s_hlo = sem("silu_done"), sem("hidden_made"), sem("hidden_high"), sem("hidden_low")
        s_mix, s_add, s_out = sem("expert_mixed"), sem("acc_updated"), sem("out_stored")

        block = ctx.enter_context(nc.Block())

        def batches(engine, core):
            core(0, 0, 0, True, False)
            with engine.Fori(0, (B - 2) // 2) as i:
                core(2 * i + 1, 1, i, False, False)
                core(2 * i + 2, 0, i + 1, False, False)
            core(B - 1, 1, (B - 1) // 2, False, True)

        def experts(engine, expert):
            expert(0, True)
            with engine.Fori(1, E) as e:
                expert(e, False)

        def chunks(engine, e, triple):
            triple(0, True)
            with engine.Fori(1, FULL // WRING) as i:
                triple(WRING * i, False)

        @block.sync
        def _(sp):
            sp.dma_start(x1[:, :, :], x.rearrange("(t p) c -> p t c", p=P)).then_inc(s_x, 16)
            sp.dma_start(cst[:, :], consts).then_inc(s_cst, 16)
            sp.dma_start(bqk_sb[:, :, :], bqk).then_inc(s_cst, 16)
            sp.dma_start(w4[:, :, :], wts).then_inc(s_w4, 16)
            sp.dma_start(bv_sb[:, :], bv.partition_broadcast(P)).then_inc(s_w4, 16)
            sp.dma_start(bo_sb[:, :], bo.partition_broadcast(P)).then_inc(s_w4, 16)

            def load_batch(b, slot):
                if not isinstance(b, int):
                    sp.wait_ge(s_task, tasks_before(b - 1, False))
                sp.dma_start(ctx_sb[slot][:, :], ctxT[:, bass.ds(b * S, S)]).then_inc(s_ctx[slot], 16)
                need(sp, s_nan, b - 1)
                sp.dma_start(mask_sb[slot][:, :, :],
                             mask[bass.ds(b * S, S), :].rearrange("(t p) k -> p t k", p=P)).then_inc(s_mask[slot], 16)

            load_batch(0, 0)
            load_batch(1, 1)
            sp.dma_start(db_sb[:, :], dbT).then_inc(s_ffnc, 16)
            sp.dma_start(rw[:, :], router).then_inc(s_ffnc, 16)
            with sp.Fori(0, (B - 2) // 2) as i:
                load_batch(2 * i + 2, 0)
                load_batch(2 * i + 3, 1)

            def load_chunk(e, c, r, before):
                need(sp, s_w, before)
                sp.dma_start(wraw[r][:, :], wfull[bass.ds((e * FULL + c) * P, P), :]).then_inc(s_raw[r], 16)

            def load_tail(e):
                need(sp, s_w, CH * e)
                sp.dma_start(wtraw[:, :], wtail[bass.ds(e * P, P), :]).then_inc(s_rawt, 16)

            def load_expert(e, first, stored):
                def triple(c, head):
                    for r in range(WRING):
                        if head:
                            load_chunk(e, c + r, r, 0 if first else CH * (e - 1) + FULL - WRING + r + 1)
                        else:
                            load_chunk(e, c + r, r, CH * e + c + r - WRING + 1)
                    if head and stored:
                        sp.wait_ge(s_wTc, 1)
                        sp.dma_start(wscratch.rearrange("(r p) -> r p", p=P), mixwT[:, :]).then_inc(s_wst, 16)
                        sp.wait_ge(s_wst, 16)
                        sp.dma_start(mixb[:, :], wscratch.partition_broadcast(P)).then_inc(s_mixb, 16)
                chunks(sp, e, triple)
                load_tail(e)

            load_expert(0, True, True)
            with sp.Fori(1, E) as e:
                load_expert(e, False, False)
            for t in range(TT):
                sp.wait_ge(s_add, TT * E + t + 1)
                sp.dma_start(out[:, t * TN:(t + 1) * TN], acc[:, t, :]).then_inc(s_out, 16)
            sp.wait_ge(s_out, 16 * TT)

        @block.gpsimd
        def _(pool):
            for s in range(2):
                pool.memset(vaug[s][:, :, :, :], 0.0).then_inc(s_psetup, 1)
            pool.wait_ge(s_psetup, 2)
            for s in range(2):
                pool.memset(vaug[s][:, :, :, DK:DK + 1], 1.0).then_inc(s_psetup, 1)
            pool.memset(expo[:, :], -0.5).then_inc(s_psetup, 1)
            pool.memset(one[:, :], 1.0).then_inc(s_psetup, 1)
            for r in range(2):
                pool.memset(htail[r][:, :].bitcast(F32), 0.0).then_inc(s_psetup, 1)
            pool.wait_ge(s_psetup, 8)
            pool.wait_ge(s_var, 1)
            pool.tensor_tensor(rstd[:, :], mv[:, :, 1], expo[:, :], ALU.pow).then_inc(s_rstd, 1)

            def qheads(b, slot):
                for g in range(G):
                    if g == 0:
                        need(pool, s_sc, UNITS * (b - 1))
                    pool.wait_ge(s_qkhi, G * b + g + 1)
                    pool.tensor_tensor(qkpack[slot][:, g, :, :], qkf[g % 2][:, :, :], qkhi[g % 2][:, :, :].bitcast(F32),
                                       ALU.subtract).then_inc(s_pack, 1)
                    pool.wait_ge(s_pack, G * b + g + 1)
                    pool.tensor_tensor(qhead[slot][:, g, :, :],
                                       qkpack[slot][:, g, 0, :].bitcast(F32).unsqueeze(1).to_broadcast([P, HG, S]),
                                       cst[:, C_HEAD:C_HEAD + HG].unsqueeze(2).to_broadcast([P, HG, S]),
                                       ALU.mult).then_inc(s_qh, 1)
                    if g == 0:
                        pool.tensor_tensor(x1[:, bass.ds(QT * b, QT), :], x1[:, bass.ds(QT * b, QT), :],
                                           bo_sb[:, :].unsqueeze(1).to_broadcast([P, QT, P]), ALU.add).then_inc(s_xb, 1)
            pool.wait_ge(s_w4, 48)
            qheads(0, 0)
            qheads(1, 1)
            with pool.Fori(0, (B - 2) // 2) as i:
                qheads(2 * i + 2, 0)
                qheads(2 * i + 3, 1)
            pool.wait_ge(s_var2, 1)
            pool.tensor_tensor(rstd[:, :], mv[:, :, 1], expo[:, :], ALU.pow).then_inc(s_rstd2, 1)

            def split(raw, hi, lo, bias, count):
                w = hi.shape[-1]
                pool.tensor_tensor(hi[:, :], raw[:, 0:w], one[:, :].to_broadcast([P, w]), ALU.mult).then_inc(s_wh, 1)
                pool.tensor_copy(bias[:, :], raw[:, w:w + 2])
                pool.wait_ge(s_wh, count)
                pool.tensor_tensor(lo[:, :], raw[:, 0:w], hi[:, :].bitcast(F32), ALU.subtract).then_inc(s_w, 1)

            def add_shares(e):
                for t in range(TT):
                    pool.wait_ge(s_mix, TT * e + t + 1)
                    pool.tensor_tensor(acc[:, t, :], acc[:, t, :], mixed[t][:, :], ALU.add).then_inc(s_add, 1)

            def expert(e, first):
                def triple(c, head):
                    for r in range(WRING):
                        pool.wait_ge(s_raw[r], 16 * (FULL // WRING * e + (0 if head else c // WRING) + 1))
                        if not head:
                            pool.wait_ge(s_down, STEPS * e + TT * (c + r - WRING) + TT)
                        elif not first:
                            pool.wait_ge(s_down, STEPS * (e - 1) + TT * (FULL - WRING + r) + TT)
                        split(wraw[r], whi[r], wlo[r], wbias[r], CH * e + c + r + 1)
                    if head and first:
                        pool.wait_ge(s_add, TT)
                    if head and not first:
                        add_shares(e - 1)
                triple(0, True)
                with pool.Fori(1, FULL // WRING) as i:
                    for r in range(WRING):
                        pool.wait_ge(s_raw[r], 16 * (FULL // WRING * e + i + 1))
                        pool.wait_ge(s_down, STEPS * e + TT * (WRING * i + r - WRING) + TT)
                        split(wraw[r], whi[r], wlo[r], wbias[r], CH * e + WRING * i + r + 1)
                pool.wait_ge(s_rawt, 16 * (e + 1))
                need(pool, s_down, STEPS * e)
                split(wtraw, wthi, wtlo, wtbias, CH * e + CH)
            experts(pool, expert)
            add_shares(E - 1)

        @block.scalar
        def _(act):
            def read_task(name, b, first, last, count, fb, fslot, bb):
                if name == "TX":
                    act.wait_ge(s_task, count)
                    act.activation(xnT[:, :], misc[:, 0:S], ACT.Copy).then_inc(s_read, 1)
                elif name[:2] == "QK":
                    g = int(name[2])
                    act.wait_ge(s_task, count)
                    need(act, s_pack, G * fb + g - 1)
                    for n in range(2):
                        ins = act.activation(qkf[g % 2][:, n, :], misc[:, n * S:(n + 1) * S], ACT.Identity,
                                             bias=bqk_sb[:, n, g:g + 1])
                    ins.then_inc(s_read, 1)
                elif name == "OT":
                    act.wait_ge(s_task, count)
                    act.activation(oT[:, :], misc[:, 0:S], ACT.Copy).then_inc(s_read, 1)

            def half1(m, parity):
                act.wait_ge(s_pt, 2 * m + 2)
                need(act, s_pv, m - 1)
                act.activation(probT[parity][:, 2:4, :, :], ptb[1][:, :], ACT.Copy).then_inc(s_pt1, 1)

            def exponentials(m, u, half):
                if half == 0:
                    act.wait_ge(s_nt, m + 1)
                    need(act, s_pt, 2 * (m - 1))
                for j in (2 * half, 2 * half + 1):
                    ins = act.activation(prob[u % 2][:, j, :], masked[u % 2][:, j, :],
                                         ACT.Exp, bias=negtop[u % 4][:, j:j + 1], scale=SCALE)
                if half == 1:
                    ins.then_inc(s_exp, 1)

            def copy_ov(count, transposed):
                act.wait_ge(s_pv, count)
                need(act, s_task, transposed)
                act.activation(ov[:, :, :], ovb[:, :], ACT.Copy).then_inc(s_ov, 1)

            def core(b, slot, k, first, last):
                order = tasks_of(first, last)
                base = tasks_before(b, first)

                def run(u, pos):
                    for n, (name, at, where) in enumerate(order):
                        if (at, where) == (u, pos):
                            read_task(name, b, first, last, base + n + 1, b + 1, 1 - slot, b - 1)
                for u in range(UNITS):
                    n = UNITS * b + u
                    if not (first and u == 0):
                        exponentials(n - 1, (u - 1) % UNITS, 0)
                    run(u, 0)
                    if not (first and u == 0):
                        exponentials(n - 1, (u - 1) % UNITS, 1)
                    if not (first and u < 2):
                        half1(n - 2, u % 2)
                    if u == 6:
                        copy_ov(UNITS * b + G, 0 if first else base + 1 + [t[0] for t in order].index("OVT1"))
                    if u == 2 and not first:
                        copy_ov(UNITS * b, base)
                    run(u, 1)

            act.wait_ge(s_cst, 32)
            for n, name in enumerate(FRONT):
                read_task(name, 0, True, False, n + 1, 0, 0, 0)
            batches(act, core)
            exponentials(UNITS * B - 1, UNITS - 1, 0)
            exponentials(UNITS * B - 1, UNITS - 1, 1)
            half1(UNITS * B - 2, 0)
            half1(UNITS * B - 1, 1)
            base = tasks_before(B - 1, False) + len(tasks_of(False, True))
            copy_ov(UNITS * B, base)
            read_task("OT", B - 1, False, True, base + 2, 0, 0, B - 1)

            for t in range(TT):
                act.wait_ge(s_x1t, t + 1)
                act.activation(acc[:, t, :], bank[2 + t % 2][:, :], ACT.Copy).then_inc(s_add, 1)
            for t in range(TT):
                act.wait_ge(s_xt, t + 1)
                act.activation(xhi[t], bank[t % 2][:, :], ACT.Copy).then_inc(s_xhi, 1)
            act.wait_ge(s_top2, 6)
            act.activation(wexp[:, :, :], lg[:, :, :], ACT.Exp).then_inc(s_rexp, 1)

            def high(c, t, step):
                act.wait_ge(s_h, step + 1)
                need(act, s_down, step - 1)
                if c == FULL:
                    act.activation(htail[t % 2][0:TAIL, :], hid[t % 2][0:TAIL, :], ACT.Copy).then_inc(s_hhi, 1)
                else:
                    act.activation(hhi[t % 2][:, :], hid[t % 2][:, :], ACT.Copy).then_inc(s_hhi, 1)

            def step(c, bias, t, number, first, before):
                rows = TAIL if c == FULL else P
                act.wait_ge(s_gate, number + 1)
                need(act, s_h, number - 1)
                act.activation(gact[t % 2][0:rows, :], bank[t % 2][0:rows, :], ACT.Silu,
                               bias=bias[0:rows, 0:1]).then_inc(s_silu, 1)
                if not first:
                    high(before, (t - 1) % TT, number - 1)

            def expert(e, head):
                def chunk(c, c_is, bias, first_chunk):
                    for t in range(TT):
                        step(c_is, bias, t, STEPS * e + TT * c + t, head and first_chunk and t == 0,
                             FULL if first_chunk and t == 0 else (c_is if t else 0))
                for r in range(WRING):
                    chunk(r, 0, wbias[r], r == 0)
                with act.Fori(1, FULL // WRING) as i:
                    for r in range(WRING):
                        chunk(WRING * i + r, 0, wbias[r], False)
                chunk(FULL, FULL, wtbias, False)
            experts(act, expert)
            high(FULL, TT - 1, STEPS * E - 1)

        @block.vector
        def _(dve):
            dve.wait_ge(s_cst, 32)
            dve.wait_ge(s_w4, 48)
            for n in range(2):
                dve.tensor_copy(wqk[:, n, :, :, :], w4[:, n, :].rearrange("p (g c) -> p g c", g=G).unsqueeze(2)
                                .to_broadcast([P, G, 4, 32])).then_inc(s_setup, 1)
            dve.wait_ge(s_x, 16)
            for t in range(TILES):
                ins = dve.bn_stats(stat[:, t, :], x1[:, t, :])
            ins.then_inc(s_stat, 1)
            dve.wait_ge(s_stat, 1)
            for t in range(TILES):
                ins = dve.bn_aggr(mv[:, t, :], stat[:, t, :])
            ins.then_inc(s_stat, 1)
            dve.wait_ge(s_stat, 2)
            dve.tensor_scalar(mv[:, :, 1], mv[:, :, 1], EPS, None, ALU.add).then_inc(s_var, 1)

            def prepare(b, slot, k):
                dve.wait_ge(s_rstd, 1)
                for qt in range(QT):
                    t = QT * b + qt
                    ins = dve.tensor_scalar(xn[:, qt, :], x1[:, bass.ds(t, 1), :], mv[:, bass.ds(t, 1), 0],
                                            rstd[:, bass.ds(t, 1)], ALU.subtract, ALU.mult)
                ins.then_inc(s_xn, 1)
                dve.wait_ge(s_mask[slot], 16 * (k + 1))
                need(dve, s_sc, UNITS * (b - 1))
                dve.tensor_scalar(maskb[slot][:, :, :], mask_sb[slot][:, :, :], 0.0, NEG, ALU.is_equal, ALU.mult).then_inc(s_mb, 1)
                dve.wait_ge(s_mb, b + 1)
                dve.tensor_reduce(mtop[slot][:, :], maskb[slot][:, :, :], AX.X, ALU.max).then_inc(s_mtop, 1)
                dve.wait_ge(s_mtop, b + 1)
                dve.tensor_scalar(nanfix[slot][:, :], mtop[slot][:, :], -NEG, 0.0, ALU.mult, ALU.mult).then_inc(s_nan, 1)

            def read_task(name, count, fb, fslot, bb):
                if name[:2] == "QK":
                    g = int(name[2])
                    dve.wait_ge(s_read, count)
                    need(dve, s_pack, G * fb + g - 1)
                    for n, col in ((0, C_LOQ), (1, C_LOK)):
                        ins = dve.tensor_scalar(qkhi[g % 2][:, n, :], qkf[g % 2][:, n, :], cst[:, col:col + 1], None, ALU.mult)
                    ins.then_inc(s_qkhi, 1)
                elif name == "V":
                    dve.wait_ge(s_task, count)
                    need(dve, s_pv, UNITS * (fb - 1))
                    dve.tensor_tensor(vaug[fslot][:, :, :, 0:DK],
                                      misc[:, 0:S].rearrange("p (t h d) -> p t h d", t=QT, d=DK),
                                      bv_sb[:, :].rearrange("p (h d) -> p h d", d=DK).unsqueeze(1).to_broadcast([P, QT, HEADS, DK]),
                                      ALU.add).then_inc(s_read, 1)
                elif name[:3] == "OVT":
                    qt = int(name[3])
                    tile = QT * (bb + 1 if qt == 0 else bb) + qt
                    dve.wait_ge(s_task, count)
                    o = misc[:, :].rearrange("p (h r) -> p h r", r=32)
                    dve.reciprocal(rden[:, :], o[:, :, DK]).then_inc(s_rden, 1)
                    dve.wait_ge(s_rden, tile + 1)
                    dve.tensor_tensor(onat[:, qt, :].rearrange("p (h d) -> p h d", d=DK), o[:, :, 0:DK],
                                      rden[:, :].unsqueeze(2).to_broadcast([P, HEADS, DK]),
                                      ALU.mult).then_inc(s_read, 1)
                elif name == "WO":
                    dve.wait_ge(s_task, count)
                    dve.wait_ge(s_xb, bb + 1)
                    tiles = bass.ds(QT * bb, QT)
                    dve.tensor_tensor(x1[:, tiles, :], misc[:, 0:S].rearrange("p (t c) -> p t c", t=QT),
                                      x1[:, tiles, :], ALU.add).then_inc(s_read, 1)
                    dve.wait_ge(s_read, count)
                    for qt in range(QT):
                        ins = dve.bn_stats(stat[:, bass.ds(QT * bb + qt, 1), :], x1[:, bass.ds(QT * bb + qt, 1), :])
                    ins.then_inc(s_stat2, 1)

            def core(b, slot, k, first, last):
                order = tasks_of(first, last)
                base = tasks_before(b, first)

                def run(u, pos):
                    for n, (name, at, where) in enumerate(order):
                        if (at, 1 if name[:2] == "QK" else where) == (u, pos):
                            read_task(name, base + n + 1, b + 1, 1 - slot, b - 1)
                for u in range(UNITS):
                    n = UNITS * b + u
                    qt = u // G
                    dve.wait_ge(s_sc, n + 1)
                    need(dve, s_exp, n - 1)
                    dve.memset(turn[:, u:u + 1], 0.0)
                    for j in range(HG):
                        ins = dve.tensor_tensor_reduce(
                            out=masked[u % 2][:, j, :], in0=scores[u % 2][j // 2][:, (j % 2) * S:(j % 2 + 1) * S],
                            in1=maskb[slot][:, qt, :], scale=1.0, scalar=LEAST, op0=ALU.add, op1=ALU.max,
                            accum_out=top[u % 4][:, j:j + 1])
                    ins.then_inc(s_top, 1)
                    run(u, 0)
                    dve.wait_ge(s_top, n + 1)
                    dve.tensor_scalar(negtop[u % 4][:, :], top[u % 4][:, :], -SCALE, nanfix[slot][:, qt:qt + 1],
                                      ALU.mult, ALU.add).then_inc(s_nt, 1)
                    if not (first and u < 2):
                        half0(n - 2, u % 2)
                    if u == 0 and not last:
                        prepare(b + 1, 1 - slot, k if slot == 0 else k + 1)
                    run(u, 1)

            def half0(m, parity):
                dve.wait_ge(s_pt, 2 * m + 1)
                need(dve, s_pv, m - 1)
                dve.tensor_copy(probT[parity][:, 0:2, :, :], ptb[0][:, :]).then_inc(s_pt0, 1)

            prepare(0, 0, 0)
            dve.wait_ge(s_psetup, 8)
            dve.wait_ge(s_w4, 48)
            for n, name in enumerate(FRONT):
                read_task(name, n + 1, 0, 0, 0)
            batches(dve, core)
            half0(UNITS * B - 2, 0)
            half0(UNITS * B - 1, 1)
            base = tasks_before(B - 1, False) + len(tasks_of(False, True))
            for n, name in enumerate(BACK):
                read_task(name, base + n + 1, 0, 0, B - 1)

            dve.wait_ge(s_stat2, B)
            for t in range(TILES):
                ins = dve.bn_aggr(mv[:, t, :], stat[:, t, :])
            ins.then_inc(s_stat2, 1)
            dve.wait_ge(s_stat2, B + 1)
            dve.tensor_scalar(mv[:, :, 1], mv[:, :, 1], EPS, None, ALU.add).then_inc(s_var2, 1)
            dve.wait_ge(s_rstd2, 1)
            for t in range(TILES):
                dve.tensor_scalar(xn2[:, t, :], x1[:, t, :], mv[:, t, 0:1], rstd[:, t:t + 1],
                                  ALU.subtract, ALU.mult).then_inc(s_xn2, 1)
            for t in range(TT):
                dve.wait_ge(s_xhi, t + 1)
                dve.tensor_copy(xf[t], bank[t % 2][:, :]).then_inc(s_xf, 1)
                dve.tensor_tensor(xlo[t], bank[t % 2][:, :], xhi[t].bitcast(F32), ALU.subtract).then_inc(s_xlo, 1)

            dve.wait_ge(s_rt, 1)
            dve.tensor_copy(lg[:, :, :], bank[4][:, 0:TILES * E].rearrange("p (t e) -> p t e", e=E)).then_inc(s_top2, 1)
            dve.wait_ge(s_top2, 1)
            other = lg[:, :, :].unsqueeze(2).to_broadcast([P, TILES, E, E])
            own = lg[:, :, :].unsqueeze(3).to_broadcast([P, TILES, E, E])
            dve.tensor_tensor(cge[:, :, :, :], other, own, ALU.is_ge).then_inc(s_top2, 1)
            dve.tensor_tensor(cgt[:, :, :, :], other, own, ALU.is_gt).then_inc(s_top2, 1)
            dve.tensor_reduce(ltop[:, :], lg[:, :, :], AX.X, ALU.max).then_inc(s_top2, 1)
            dve.wait_ge(s_top2, 4)
            before = cst[:, C_GE:C_GE + E * E].rearrange("p (e f) -> p e f", f=E).unsqueeze(1).to_broadcast([P, TILES, E, E])
            after = cst[:, C_GT:C_GT + E * E].rearrange("p (e f) -> p e f", f=E).unsqueeze(1).to_broadcast([P, TILES, E, E])
            dve.tensor_tensor(lg[:, :, :], lg[:, :, :], ltop[:, :].unsqueeze(2).to_broadcast([P, TILES, E]),
                              ALU.subtract).then_inc(s_top2, 1)
            dve.tensor_tensor(cge[:, :, :, :], cge[:, :, :, :], before, ALU.mult).then_inc(s_top2, 1)
            dve.tensor_tensor(cgt[:, :, :, :], cgt[:, :, :, :], after, ALU.mult).then_inc(s_top2, 1)
            dve.wait_ge(s_top2, 7)
            dve.tensor_tensor(cge[:, :, :, :], cge[:, :, :, :], cgt[:, :, :, :], ALU.add).then_inc(s_top2, 1)
            dve.wait_ge(s_top2, 8)
            dve.tensor_reduce(rank[:, :, :], cge[:, :, :, :], AX.X, ALU.add).then_inc(s_top2, 1)
            dve.wait_ge(s_top2, 9)
            dve.wait_ge(s_rexp, 1)
            dve.scalar_tensor_tensor(out=rank[:, :, :], in0=rank[:, :, :], scalar=1.5, in1=wexp[:, :, :],
                                     op0=ALU.is_lt, op1=ALU.mult).then_inc(s_top2, 1)
            dve.wait_ge(s_top2, 10)
            dve.tensor_reduce(wsum[:, :], rank[:, :, :], AX.X, ALU.add).then_inc(s_top2, 1)
            dve.wait_ge(s_top2, 11)
            dve.reciprocal(ltop[:, :], wsum[:, :]).then_inc(s_top2, 1)
            dve.wait_ge(s_top2, 12)
            dve.tensor_tensor(mixw[:, :, :].rearrange("p e t -> p t e"), rank[:, :, :],
                              ltop[:, :].unsqueeze(2).to_broadcast([P, TILES, E]), ALU.mult).then_inc(s_top2, 1)
            dve.wait_ge(s_wT, 1)
            dve.tensor_copy(mixwT[:, :], bank[5][0:E * TILES, 0:P]).then_inc(s_wTc, 1)
            dve.wait_ge(s_ffnc, 32)

            def low(c, t, step):
                dve.wait_ge(s_hhi, step + 1)
                need(dve, s_down, step - 1)
                if c == FULL:
                    dve.tensor_tensor(htail[t % 2][UP0:UP0 + TAIL, :], hid[t % 2][0:TAIL, :],
                                      htail[t % 2][0:TAIL, :].bitcast(F32), ALU.subtract).then_inc(s_hlo, 1)
                else:
                    dve.tensor_tensor(hlo[t % 2][:, :], hid[t % 2][:, :], hhi[t % 2][:, :].bitcast(F32),
                                      ALU.subtract).then_inc(s_hlo, 1)

            def mix(e, t):
                dve.wait_ge(s_down, STEPS * e + TT * FULL + t + 1)
                if t == 0:
                    dve.wait_ge(s_mixb, 16)
                dve.wait_ge(s_add, TT * e + t + 1)
                dve.scalar_tensor_tensor(out=mixed[t][:, :], in0=bank[4 + t][:, :], scalar=db_sb[:, bass.ds(e, 1)],
                                         in1=mixb[:, bass.ds(e * TOK + t * TN, TN)], op0=ALU.add,
                                         op1=ALU.mult).then_inc(s_mix, 1)

            def step(c_is, bias, t, number, ups, first, before):
                dve.wait_ge(s_silu, number + 1)
                need(dve, s_hlo, number - 1)
                if c_is == FULL:
                    dve.scalar_tensor_tensor(out=hid[t % 2][0:TAIL, :], in0=bank[t % 2][UP0:UP0 + TAIL, :],
                                             scalar=bias[UP0:UP0 + TAIL, 1:2],
                                             in1=gact[t % 2][0:TAIL, :], op0=ALU.add, op1=ALU.mult).then_inc(s_h, 1)
                else:
                    dve.wait_ge(s_up, ups)
                    dve.scalar_tensor_tensor(out=hid[t % 2][:, :], in0=bank[2 + t % 2][:, :],
                                             scalar=bias[:, 1:2], in1=gact[t % 2][:, :],
                                             op0=ALU.add, op1=ALU.mult).then_inc(s_h, 1)
                if not first:
                    low(before, (t - 1) % TT, number - 1)

            def expert(e, head):
                def chunk(c, c_is, bias, first_chunk):
                    for t in range(TT):
                        step(c_is, bias, t, STEPS * e + TT * c + t, (STEPS - TT) * e + TT * c + t + 1, head and first_chunk and t == 0,
                             FULL if first_chunk and t == 0 else (c_is if t else 0))
                        if first_chunk and not head:
                            mix(e - 1, t)
                for r in range(WRING):
                    chunk(r, 0, wbias[r], r == 0)
                with dve.Fori(1, FULL // WRING) as i:
                    for r in range(WRING):
                        chunk(WRING * i + r, 0, wbias[r], False)
                chunk(FULL, FULL, wtbias, False)
            experts(dve, expert)
            low(FULL, TT - 1, STEPS * E - 1)
            for t in range(TT):
                mix(E - 1, t)

        @block.tensor
        def _(pe):
            def run_task(name, count, fb, fslot, fk, bb, bslot):
                need(pe, s_read, count - 1)
                if name == "TX":
                    pe.wait_ge(s_xn, fb + 1)
                    for qt in range(QT):
                        ins = pe.transpose(misc[:, qt * P:(qt + 1) * P], xn[:, qt, :], ident)
                    ins.then_inc(s_task, 1)
                elif name[:2] == "QK":
                    g = int(name[2])
                    pe.wait_ge(s_ctx[fslot], 16 * (fk + 1))
                    for n, moving in ((0, xnT), (1, ctx_sb[fslot])):
                        ins = pe.matmul(misc[:, n * S:(n + 1) * S], wqk[:, n, g, :, :].rearrange("p q c -> p (q c)"), moving[:, :], start=True, stop=True)
                    ins.then_inc(s_task, 1)
                elif name == "V":
                    for kt in range(QT):
                        ins = pe.matmul(misc[:, kt * P:(kt + 1) * P], ctx_sb[fslot][:, kt * P:(kt + 1) * P], w4[:, 2, :],
                                        start=True, stop=True)
                    ins.then_inc(s_task, 1)
                elif name[:3] == "OVT":
                    qt = int(name[3])
                    pe.wait_ge(s_ov, QT * (bb + 1 if qt == 0 else bb) + qt + 1)
                    for g in range(G):
                        ins = pe.transpose(misc[:, g * P:(g + 1) * P], ov[:, g, :], ident)
                    ins.then_inc(s_task, 1)
                elif name == "OT":
                    for qt in range(QT):
                        ins = pe.transpose(misc[:, qt * P:(qt + 1) * P], onat[:, qt, :], ident)
                    ins.then_inc(s_task, 1)
                elif name == "WO":
                    for qt in range(QT):
                        ins = pe.matmul(misc[:, qt * P:(qt + 1) * P], oT[:, qt * P:(qt + 1) * P], w4[:, 3, :],
                                        start=True, stop=True)
                    ins.then_inc(s_task, 1)

            def score(b, slot, u):
                n = UNITS * b + u
                qt, g = u // G, u % G
                if qt == 0:
                    pe.wait_ge(s_qh, G * b + g + 1)
                need(pe, s_top, n - 1)
                for j in range(HG):
                    ins = pe.matmul(scores[u % 2][j // 2][:, (j % 2) * S:(j % 2 + 1) * S],
                                    qhead[slot][:, g, j, qt * P:(qt + 1) * P], qkpack[slot][:, g, 1, :],
                                    start=True, stop=True)
                ins.then_inc(s_sc, 1)

            def transpose_probs(m, parity):
                pe.wait_ge(s_exp, m + 1)
                for half, copied in ((0, s_pt0), (1, s_pt1)):
                    need(pe, copied, m)
                    for j in range(2):
                        for kt in range(QT):
                            ins = pe.transpose(ptb[half][:, (2 * j + kt) * P:(2 * j + kt + 1) * P],
                                               prob[parity][:, 2 * half + j, kt * P:(kt + 1) * P], ident)
                    ins.then_inc(s_pt, 1)

            def weigh_values(m, slot, u, tiles):
                g = u % G
                pe.wait_ge(s_pt0, m + 1)
                pe.wait_ge(s_pt1, m + 1)
                if g == 0:
                    need(pe, s_ov, tiles)
                for kt in range(QT):
                    for j in range(HG):
                        ins = pe.matmul(ovb[32 * j:32 * j + 32, g * P:(g + 1) * P], vaug[slot][:, kt, HG * g + j, :],
                                        probT[u % 2][:, j, kt, :], start=kt == 0, stop=kt == QT - 1)
                ins.then_inc(s_pv, 1)

            def core(b, slot, k, first, last):
                order = tasks_of(first, last)
                base = tasks_before(b, first)
                fk = k if slot == 0 else k + 1

                def run(u, pos):
                    for n, (name, at, where) in enumerate(order):
                        if (at, where) == (u, pos):
                            run_task(name, base + n + 1, b + 1, 1 - slot, fk, b - 1, 1 - slot)
                for u in range(UNITS):
                    n = UNITS * b + u
                    score(b, slot, u)
                    run(u, 0)
                    if not (first and u < 2):
                        transpose_probs(n - 2, u % 2)
                    if u == 3:
                        pe.wait_ge(s_read, base)
                    if not (first and u < 3):
                        weigh_values(n - 3, slot if u >= 3 else 1 - slot, (u - 3) % UNITS,
                                     QT * b + (u - 3) // G)
                    run(u, 1)

            pe.wait_ge(s_cst, 32)
            pe.wait_ge(s_w4, 48)
            pe.wait_ge(s_setup, 2)
            pe.wait_ge(s_psetup, 8)
            for n, name in enumerate(FRONT):
                run_task(name, n + 1, 0, 0, 0, 0, 0)
            batches(pe, core)
            last = UNITS * B
            transpose_probs(last - 2, 0)
            weigh_values(last - 3, 1, UNITS - 3, 0)
            transpose_probs(last - 1, 1)
            weigh_values(last - 2, 1, UNITS - 2, 0)
            weigh_values(last - 1, 1, UNITS - 1, 0)
            base = tasks_before(B - 1, False) + len(tasks_of(False, True))
            for n, name in enumerate(BACK):
                run_task(name, base + n + 1, 0, 0, 0, B - 1, 1)

            pe.wait_ge(s_read, base + len(BACK))
            for t in range(TT):
                need(pe, s_add, t - 1)
                for n in range(TN // P):
                    ins = pe.transpose(bank[2 + t % 2][:, n * P:(n + 1) * P], x1[:, TN // P * t + n, :], ident)
                ins.then_inc(s_x1t, 1)
            for t in range(TT):
                need(pe, s_xlo, t - 1)
                pe.wait_ge(s_xn2, TN // P * (t + 1))
                for n in range(TN // P):
                    ins = pe.transpose(bank[t % 2][:, n * P:(n + 1) * P], xn2[:, TN // P * t + n, :], ident)
                ins.then_inc(s_xt, 1)
            pe.wait_ge(s_ffnc, 32)
            for t in range(TILES):
                pe.wait_ge(s_xf, t // (TN // P) + 1)
                ins = pe.matmul(bank[4][:, t * E:(t + 1) * E], xf[t // (TN // P)][:, (t % (TN // P)) * P:(t % (TN // P) + 1) * P],
                                rw[:, :], start=True, stop=True)
            ins.then_inc(s_rt, 1)
            pe.wait_ge(s_top2, 13)
            pe.transpose(bank[5][0:E * TILES, 0:P], mixw[:, :, :], ident).then_inc(s_wT, 1)
            pe.wait_ge(s_wTc, 1)
            pe.wait_ge(s_xlo, TT)

            def up_products(dst, hi, lo, t):
                pe.matmul(dst, hi, xhi[t], start=True, stop=False)
                pe.matmul(dst, hi, xlo[t], start=False, stop=False)
                return pe.matmul(dst, lo, xhi[t], start=False, stop=True)

            def down(c_is, r, t, number, start, mixed_before):
                pe.wait_ge(s_hlo, number + 1)
                if start:
                    need(pe, s_mix, mixed_before)
                dst = bank[4 + t][:, :]
                if c_is == FULL:
                    pe.matmul(dst, wthi[:, P:2 * P], htail[t % 2][:, :], start=False, stop=False)
                    pe.matmul(dst, wtlo[:, P:2 * P], htail[t % 2][:, :], start=False, stop=True).then_inc(s_down, 1)
                else:
                    hi, lo = whi[r][:, 2 * P:3 * P], wlo[r][:, 2 * P:3 * P]
                    pe.matmul(dst, hi, hhi[t % 2][:, :], start=start, stop=False)
                    pe.matmul(dst, hi, hlo[t % 2][:, :], start=False, stop=False)
                    pe.matmul(dst, lo, hhi[t % 2][:, :], start=False, stop=False).then_inc(s_down, 1)

            def expert(e, head):
                def chunk(c, c_is, r, kind):
                    for t in range(TT):
                        number = STEPS * e + TT * c + t
                        if t == 0:
                            pe.wait_ge(s_w, CH * e + c + 1)
                        need(pe, s_silu, number - 1)
                        if c_is == FULL:
                            up_products(bank[t % 2][:, :], wthi[:, 0:P], wtlo[:, 0:P], t).then_inc(s_gate, 1)
                        else:
                            need(pe, s_h, number - 1)
                            up_products(bank[t % 2][:, :], whi[r][:, 0:P], wlo[r][:, 0:P], t).then_inc(s_gate, 1)
                            up_products(bank[2 + t % 2][:, :], whi[r][:, P:2 * P], wlo[r][:, P:2 * P], t).then_inc(s_up, 1)
                        td = (t - LAG) % TT
                        if t >= LAG:
                            down(c_is, r, td, number - LAG, kind == 0, 0 if head else TT * (e - 1) + td + 1)
                        elif kind == 0:
                            if not head:
                                down(FULL, 0, td, number - LAG, False, 0)
                        else:
                            down(0, (r - 1) % WRING, td, number - LAG, kind == 1, 0 if head else TT * (e - 1) + td + 1)
                for r in range(WRING):
                    chunk(r, 0, r, r)
                with pe.Fori(1, FULL // WRING) as i:
                    for r in range(WRING):
                        chunk(WRING * i + r, 0, r, 2)
                chunk(FULL, FULL, 0, 2)
            experts(pe, expert)
            for t in range(TT - LAG, TT):
                down(FULL, 0, t, STEPS * (E - 1) + TT * FULL + t, False, 0)


def kernel(x, ctx_1024, mask_BxSxS2_ik0, L0_xattn_wq, L0_xattn_bq, L0_xattn_wk, L0_xattn_bk, L0_xattn_wv,
           L0_xattn_bv, L0_xattn_wo, L0_xattn_bo, L0_ffn_gate_w, L0_ffn_gate_b, L0_ffn_up_w, L0_ffn_up_b,
           L0_ffn_down_w, L0_ffn_down_b, L0_ffn_router_w):
    import numpy as np
    import concourse.bacc as bacc
    from concourse.bass_utils import run_bass_kernel_spmd

    a = lambda v: np.asarray(v)
    x, ctxv, mask = a(x), a(ctx_1024), a(mask_BxSxS2_ik0)
    gw, uw, dw = a(L0_ffn_gate_w), a(L0_ffn_up_w), a(L0_ffn_down_w)
    gb, ub = a(L0_ffn_gate_b), a(L0_ffn_up_b)
    cut = FULL * P

    consts = np.zeros((P, C_N), np.float32)
    consts[:, C_ID:C_ID + P] = np.eye(P)
    row = np.arange(P)
    consts[:, C_LOQ] = (row // 32) % 2
    consts[:, C_LOK] = row // 64
    for j in range(HG):
        consts[:, C_HEAD + j] = (row % 32) // DK == j
    earlier = np.tril(np.ones((E, E)), -1)
    consts[:, C_GE:C_GE + E * E] = earlier.reshape(1, -1)
    consts[:, C_GT:C_GT + E * E] = earlier.T.reshape(1, -1)

    wts = np.stack([a(w).T for w in (L0_xattn_wq, L0_xattn_wk, L0_xattn_wv, L0_xattn_wo)], 1)
    bqk = np.stack([np.concatenate([a(b).reshape(G, 32).T] * 4) for b in (L0_xattn_bq, L0_xattn_bk)], 1)
    gate = gw[:, :, :cut].reshape(E, P, FULL, P).transpose(0, 2, 1, 3)
    up = uw[:, :, :cut].reshape(E, P, FULL, P).transpose(0, 2, 1, 3)
    dn = dw[:, :cut].reshape(E, FULL, P, P)
    biases = [b[:, :cut].reshape(E, FULL, P, 1) for b in (gb, ub)]
    wfull = np.concatenate([gate, up, dn] + biases, 3).reshape(E * FULL * P, 3 * P + 2)
    wtail = np.zeros((E, P, 2 * P + 2), np.float32)
    wtail[:, :, 0:TAIL] = gw[:, :, cut:]
    wtail[:, :, UP0:UP0 + TAIL] = uw[:, :, cut:]
    wtail[:, 0:TAIL, P:2 * P] = dw[:, cut:]
    wtail[:, UP0:UP0 + TAIL, P:2 * P] = dw[:, cut:]
    wtail[:, 0:TAIL, 2 * P] = gb[:, cut:]
    wtail[:, UP0:UP0 + TAIL, 2 * P + 1] = ub[:, cut:]

    arrays = {
        "x": x.reshape(TOK, D),
        "ctxT": ctxv.reshape(TOK, D).T,
        "mask": mask.reshape(TOK, S),
        "wts": wts, "bqk": bqk, "bv": a(L0_xattn_bv), "bo": a(L0_xattn_bo), "consts": consts,
        "wfull": wfull, "wtail": wtail.reshape(E * P, 2 * P + 2),
        "dbT": a(L0_ffn_down_b).T, "router": a(L0_ffn_router_w),
    }
    nc = bacc.Bacc("TRN2", target_bir_lowering=False, num_devices=1)
    fed, args = {}, []
    for name, v in arrays.items():
        v = np.ascontiguousarray(v)
        fed[f"in_{name}"] = v
        args.append(nc.dram_tensor(f"in_{name}", v.shape, mybir.dt.from_np(v.dtype), kind="ExternalInput").ap())
    args.append(nc.dram_tensor("mixw_scratch", (E * TOK,), F32, kind="Internal").ap())
    args.append(nc.dram_tensor("outT", (P, TOK), F32, kind="ExternalOutput").ap())
    program(nc, *args)
    r = run_bass_kernel_spmd(nc, [fed], core_ids=[0])
    return r.results[0]["outT"].T.reshape(B, S, D)
```

```python
from contextlib import ExitStack
import math

import concourse.bass as bass
from concourse import mybir
from concourse.alu_op_type import AluOpType as ALU

ACT = mybir.ActivationFunctionType
AX = mybir.AxisListType
F32, F32R, BF16, I32 = mybir.dt.float32, mybir.dt.float32r, mybir.dt.bfloat16, mybir.dt.int32

P = 128
B, S, D = 8, 256, 128
HEADS, DK = 16, 8
QT = S // P
G = 4
HG = HEADS // G
UNITS = QT * G
TOK = B * S
TILES = TOK // P
E, H = 4, 2730
FULL = H // P
TAIL = H - FULL * P
CH = FULL + 1
WRING = 3
TN = 512
TT = TOK // TN
GT = TN // P
STEPS = CH * TT
LAG = 2
UP0 = 64
SCALE = float(DK) ** -0.5
NEG = -3e38
NO_KEY = 1e38
EPS = 1e-5
C_ID, C_LOQ, C_LOK, C_HEAD, C_GE, C_GT, C_N = 0, P, P + 1, P + 2, P + 6, P + 22, P + 38
TASKS = [("TX", 1, 0), ("QK0", 2, 0), ("QK1", 3, 0), ("OVT1", 3, 2), ("QK2", 4, 2),
         ("OT", 5, 2), ("WO", 6, 0), ("QK3", 6, 2), ("V", 7, 0), ("OVT0", 7, 2)]
FRONT = ["TX", "QK0", "QK1", "QK2", "QK3", "V"]
POOL_LESS = G // 2
BACK = ["OVT1", "OT", "WO"]
EARLY = 3
TOP_LOGITS, TOP_WEIGHTS = 11, 16
LAST_TASKS = [("X1T0", 0, 0), ("X1T1", 1, 0), ("X1T2", 2, 0), ("XT0", 3, 0), ("OVT1", 3, 2), ("XT1", 4, 2),
              ("OT", 5, 2), ("WO", 6, 0), ("XT2", 6, 2), ("OVT0", 7, 2)]
FRONT_TASKS = ["TX", "QK0", "QK1", "V", "QK2", "QK3"]


def tasks_of(first, last):
    return LAST_TASKS if last else [t for t in TASKS if not (first and t[0] in BACK)]


def tasks_before(b, first):
    return 0 if first else len(TASKS) * b + len(tasks_of(True, False)) - len(TASKS)


def need(engine, sem, value):
    if not isinstance(value, int) or value > 0:
        engine.wait_ge(sem, value)


def program(nc, x, ctxT, mask, wts, bqk, bv, bo, consts, wfull, wtail, dbT, router, wscratch, out):
    ctx = ExitStack()
    with ctx:
        def sb(name, shape, dt=F32):
            return ctx.enter_context(nc.sbuf_tensor(name, shape, dt))

        def sem(name):
            return ctx.enter_context(nc.semaphore(name))

        cst = sb("cst", [P, C_N])
        ident = cst[:, C_ID:C_ID + P]
        w4 = sb("w4", [P, 4, P])
        wqk = sb("wqk", [P, 2, G, 4, 32])
        bqk_sb = sb("bqk_sb", [P, 2, G])
        bv_sb = sb("bv_sb", [P, P])
        bo_sb = sb("bo_sb", [P, P])
        x1 = sb("x1", [P, TILES, P])
        stat = sb("stat", [P, TILES, 6])
        mv = sb("mv", [P, TILES, 2])
        rstd = sb("rstd", [P, TILES])
        expo = sb("expo", [P, TILES])
        one = sb("one", [P, 1])
        first = sb("first", [P, 1])
        xn = sb("xn", [P, QT, P])
        xnT = sb("xnT", [P, S])
        ctx_sb = [sb(f"ctx{s}", [P, S]) for s in range(2)]
        mask_sb = [sb(f"mask{s}", [P, QT, S], I32) for s in range(2)]
        maskb = [sb(f"maskb{s}", [P, QT, S], BF16) for s in range(2)]
        qkf = [sb(f"qkf{r}", [P, 2, S]) for r in range(2)]
        qkhi = [sb(f"qkhi{r}", [P, 2, S], F32R) for r in range(2)]
        qkpack = [sb(f"qkpack{s}", [P, G, 2, S], F32R) for s in range(2)]
        qhead = [sb(f"qhead{s}", [P, G, HG, S], F32R) for s in range(2)]
        vaug = [sb(f"vaug{s}", [P, QT, HEADS, 32]) for s in range(2)]
        turn = sb("turn", [P, UNITS])
        negtop = [sb(f"negtop{r}", [P, HG]) for r in range(4)]
        masked = [sb(f"masked{r}", [P, HG, S]) for r in range(2)]
        prob = [sb(f"prob{r}", [P, HG, S]) for r in range(2)]
        probT = [sb(f"probT{r}", [P, HG, QT, P]) for r in range(2)]
        ov = sb("ov", [P, G, P])
        rden = sb("rden", [P, HEADS])
        onat = sb("onat", [P, QT, P])
        oT = sb("oT", [P, S])
        xn2 = sb("xn2", [P, TILES, P])
        acc = sb("acc", [P, TT, TN])
        rw = sb("rw", [P, E])
        rsplit = sb("rsplit", [P, 2, E], F32R)
        euler = sb("euler", [P, TILES])
        second = sb("second", [P, TILES])
        share = sb("share", [P, TILES])
        lg = sb("lg", [P, TILES, E])
        cge = sb("cge", [P, TILES, E, E])
        cgt = sb("cgt", [P, TILES, E, E])
        rank = sb("rank", [P, TILES, E])
        ltop = sb("ltop", [P, TILES])
        wexp = sb("wexp", [P, TILES, E])
        wsum = sb("wsum", [P, TILES])
        mixw = sb("mixw", [P, E, TILES])
        mixwT = sb("mixwT", [E * TILES, P])
        mixb = sb("mixb", [P, E * TOK])
        db_sb = sb("db_sb", [P, E])
        wraw = [sb(f"wraw{r}", [P, 3 * P + 2]) for r in range(WRING)]
        whi = [sb(f"whi{r}", [P, 3 * P], F32R) for r in range(WRING)]
        wlo = [sb(f"wlo{r}", [P, 3 * P], F32R) for r in range(WRING)]
        wtraw = sb("wtraw", [P, 2 * P + 2])
        wbias = [sb(f"wbias{r}", [P, 2]) for r in range(WRING)]
        wtbias = sb("wtbias", [P, 2])
        wthi = sb("wthi", [P, 2 * P], F32R)
        wtlo = sb("wtlo", [P, 2 * P], F32R)
        xhalves = qhead[0][:, :, :, :].rearrange("p g h s -> p (g h s)")
        xhi, xlo = ([xhalves[:, (TT * half + t) * TN:(TT * half + t + 1) * TN] for t in range(TT)] for half in range(2))
        flat = [v[:, :, :].rearrange("p h k -> p (h k)") for v in prob] + \
               [v[:, :, :, :].rearrange("p h t q -> p (h t q)") for v in probT]
        gact, hid = ([f[:, n * TN:(n + 1) * TN] for n in range(2)] for f in flat[2:4])
        hhi = [sb(f"hhi{r}", [P, TN], F32R) for r in range(2)]
        hlo = [sb(f"hlo{r}", [P, TN], F32R) for r in range(2)]
        htail = [sb(f"htail{r}", [P, TN], F32R) for r in range(2)]
        mixed = [flat[t // 2][:, t % 2 * TN:(t % 2 + 1) * TN] for t in range(TT)]

        bank = [ctx.enter_context(nc.psum_tensor(f"bank{n}", [P, TN], F32)) for n in range(8)]
        scores = [[bank[0], bank[1]], [bank[2], bank[3]]]
        ptb, ovb, misc = [bank[4], bank[5]], bank[6], bank[7]
        front_bank, front_v = [bank[0], bank[4], bank[5], bank[6]], bank[2]

        s_cst, s_x, s_w4 = sem("cst_loaded"), sem("x_loaded"), sem("w4_loaded")
        s_ffnc = sem("ffn_consts_loaded")
        s_ctx = [sem(f"ctx_loaded{s}") for s in range(2)]
        s_mask = [sem(f"mask_loaded{s}") for s in range(2)]
        s_x0, s_xsecond, s_bqk, s_bvo = sem("first_x_loaded"), sem("second_x_loaded"), sem("bqk_loaded"), sem("bv_bo_loaded")
        s_wqk, s_psetup = sem("wqk_copied"), sem("pool_setup_done")
        s_qkhi0, s_pack0, s_qh0 = sem("first_high_rows"), sem("first_packed"), sem("first_qhead")
        s_front, s_front_read, s_xnT0, s_v0 = (sem("front_task_done"), sem("front_qk_copied"),
                                               sem("first_xnT_copied"), sem("first_values_made"))
        s_stat, s_var, s_rstd = sem("stats_made"), sem("variance_made"), sem("rstd_made")
        s_xb, s_xn = sem("bias_added"), sem("xn_made")
        s_mb = sem("maskb_made")
        s_task, s_read = sem("task_done"), sem("task_read")
        s_qkhi, s_pack, s_qh = sem("qk_high_rows_made"), sem("qk_packed"), sem("qhead_made")
        s_sc, s_top = sem("scores_done"), sem("top_made")
        s_exp, s_pt = sem("probs_made"), sem("probs_transposed")
        s_pt0, s_pt1 = sem("half0_copied"), sem("half1_copied")
        s_pv, s_ov = sem("values_weighted"), sem("ov_copied")
        s_rden = sem("rden_made")
        s_rsplit, s_centred = sem("router_split"), sem("xn2_centred")
        s_stat2, s_aggr2, s_var2 = sem("stats2_made"), sem("stats2_aggregated"), sem("variance2_made")
        s_rstd2, s_xn2 = sem("rstd2_made"), sem("xn2_made")
        s_xt, s_x1t = sem("last_xn2_transposed"), sem("last_x1_transposed")
        s_xhi, s_xlo = sem("xhi_made"), sem("last_xlo_made")
        s_rt, s_top2, s_rexp = sem("routed"), sem("router_vector_step"), sem("router_exp")
        s_wT, s_wTc, s_wst, s_mixb = sem("mixw_transposed"), sem("mixwT_copied"), sem("mixw_stored"), sem("mixb_loaded")
        s_raw = [sem(f"wraw_loaded{r}") for r in range(WRING)]
        s_rawt = sem("wtail_loaded")
        s_wh, s_w = sem("weights_high_made"), sem("weights_split")
        s_gate, s_up, s_down = sem("gate_done"), sem("up_done"), sem("down_done")
        s_silu, s_h, s_hhi, s_hlo = sem("silu_done"), sem("hidden_made"), sem("hidden_high"), sem("hidden_low")
        s_mix, s_add, s_addlast, s_out = sem("expert_mixed"), sem("acc_updated"), sem("last_acc_updated"), sem("out_stored")

        block = ctx.enter_context(nc.Block())

        def grouped(engine):
            def high_rows(g):
                return engine.tensor_tensor(qkhi[g % 2][:, :, :], qkf[g % 2][:, :, :],
                                            cst[:, C_LOQ:C_LOQ + 2].unsqueeze(2).to_broadcast([P, 2, S]), ALU.mult)

            def packed(slot, g):
                return engine.tensor_tensor(qkpack[slot][:, g, :, :], qkf[g % 2][:, :, :],
                                            qkhi[g % 2][:, :, :].bitcast(F32), ALU.subtract)

            def by_head(slot, g):
                return engine.tensor_tensor(qhead[slot][:, g, :, :],
                                            qkpack[slot][:, g, 0, :].bitcast(F32).unsqueeze(1).to_broadcast([P, HG, S]),
                                            cst[:, C_HEAD:C_HEAD + HG].unsqueeze(2).to_broadcast([P, HG, S]), ALU.mult)
            return high_rows, packed, by_head

        def batches(engine, core):
            core(0, 0, 0, True, False)
            with engine.Fori(0, (B - 2) // 2) as i:
                core(2 * i + 1, 1, i, False, False)
                core(2 * i + 2, 0, i + 1, False, False)
            core(B - 1, 1, (B - 1) // 2, False, True)

        def experts(engine, expert):
            expert(0, True)
            with engine.Fori(1, E) as e:
                expert(e, False)

        @block.sync
        def _(sp):
            by_tile = x.rearrange("(t p) c -> p t c", p=P)
            sp.dma_start(x1[:, 0:QT, :], by_tile[:, 0:QT, :]).then_inc(s_x0, 16)
            sp.dma_start(w4[:, :, :], wts).then_inc(s_w4, 16)
            sp.dma_start(x1[:, QT:2 * QT, :], by_tile[:, QT:2 * QT, :]).then_inc(s_xsecond, 16)
            sp.dma_start(ctx_sb[0][:, :], ctxT[:, 0:S]).then_inc(s_ctx[0], 16)
            sp.dma_start(cst[:, :], consts).then_inc(s_cst, 16)
            sp.dma_start(bqk_sb[:, :, :], bqk).then_inc(s_bqk, 16)
            sp.dma_start(x1[:, 2 * QT:TILES, :], by_tile[:, 2 * QT:TILES, :]).then_inc(s_x, 16)
            sp.dma_start(mask_sb[0][:, :, :], mask[0:S, :].rearrange("(t p) k -> p t k", p=P)).then_inc(s_mask[0], 16)
            sp.dma_start(bv_sb[:, :], bv.partition_broadcast(P)).then_inc(s_bvo, 16)
            sp.dma_start(bo_sb[:, :], bo.partition_broadcast(P)).then_inc(s_bvo, 16)

            def load_batch(b, slot):
                if not isinstance(b, int):
                    sp.wait_ge(s_task, tasks_before(b - 1, False))
                sp.dma_start(ctx_sb[slot][:, :], ctxT[:, bass.ds(b * S, S)]).then_inc(s_ctx[slot], 16)
                need(sp, s_mb, b - 1)
                sp.dma_start(mask_sb[slot][:, :, :],
                             mask[bass.ds(b * S, S), :].rearrange("(t p) k -> p t k", p=P)).then_inc(s_mask[slot], 16)

            load_batch(1, 1)
            sp.dma_start(db_sb[:, :], dbT).then_inc(s_ffnc, 16)
            sp.dma_start(rw[:, :], router).then_inc(s_ffnc, 16)
            with sp.Fori(0, (B - 2) // 2) as i:
                load_batch(2 * i + 2, 0)
                load_batch(2 * i + 3, 1)

            def load_chunk(e, c, r, before):
                need(sp, s_w, before)
                sp.dma_start(wraw[r][:, :], wfull[bass.ds((e * FULL + c) * P, P), :]).then_inc(s_raw[r], 16)

            def load_tail(e):
                need(sp, s_w, CH * e)
                sp.dma_start(wtraw[:, :], wtail[bass.ds(e * P, P), :]).then_inc(s_rawt, 16)

            def load_triple(e, c, head, first):
                for r in range(WRING):
                    if head:
                        load_chunk(e, c + r, r, 0 if first else CH * (e - 1) + FULL - WRING + r + 1)
                    else:
                        load_chunk(e, c + r, r, CH * e + c + r - WRING + 1)

            load_triple(0, 0, True, True)
            load_triple(0, WRING, False, True)
            sp.wait_ge(s_wTc, 1)
            sp.dma_start(wscratch.rearrange("(r p) -> r p", p=P), mixwT[:, :]).then_inc(s_wst, 16)
            sp.wait_ge(s_wst, 16)
            sp.dma_start(mixb[:, :], wscratch.partition_broadcast(P)).then_inc(s_mixb, 16)
            with sp.Fori(2, FULL // WRING) as i:
                load_triple(0, WRING * i, False, True)
            load_tail(0)
            with sp.Fori(1, E) as e:
                load_triple(e, 0, True, False)
                with sp.Fori(1, FULL // WRING) as i:
                    load_triple(e, WRING * i, False, False)
                load_tail(e)
            for t in range(TT):
                if t < TT // 2:
                    sp.wait_ge(s_add, TT * E + t + 1)
                else:
                    sp.wait_ge(s_addlast, t - TT // 2 + 1)
                sp.dma_start(out[:, t * TN:(t + 1) * TN], acc[:, t, :]).then_inc(s_out, 16)
            sp.wait_ge(s_out, 16 * TT)

        @block.gpsimd
        def _(pool):
            pool.memset(expo[:, :], -0.5).then_inc(s_psetup, 1)
            pool.memset(vaug[0][:, :, :, :], 0.0).then_inc(s_psetup, 1)
            pool.wait_ge(s_psetup, 2)
            pool.memset(vaug[0][:, :, :, DK:DK + 1], 1.0).then_inc(s_psetup, 1)

            def reciprocal_deviations(t0, t1, count):
                pool.wait_ge(s_var, count)
                pool.tensor_tensor(rstd[:, t0:t1], mv[:, t0:t1, 1], expo[:, t0:t1], ALU.pow).then_inc(s_rstd, 1)

            reciprocal_deviations(0, QT, 1)
            reciprocal_deviations(QT, 2 * QT, 2)
            pool.memset(one[:, :], 1.0).then_inc(s_psetup, 1)
            pool.memset(euler[:, :], math.e)
            pool.memset(vaug[1][:, :, :, :], 0.0).then_inc(s_psetup, 1)
            pool.wait_ge(s_psetup, 5)
            pool.memset(vaug[1][:, :, :, DK:DK + 1], 1.0).then_inc(s_psetup, 1)

            high_rows, packed, by_head = grouped(pool)

            def add_bias(b):
                pool.tensor_tensor(x1[:, bass.ds(QT * b, QT), :], x1[:, bass.ds(QT * b, QT), :],
                                   bo_sb[:, :].unsqueeze(1).to_broadcast([P, QT, P]), ALU.add).then_inc(s_xb, 1)

            pool.wait_ge(s_cst, 16)
            for n, g in enumerate((1, 3)):
                pool.wait_ge(s_front_read, g + 1)
                high_rows(g).then_inc(s_qkhi, 1)
                pool.wait_ge(s_qkhi, n + 1)
                packed(0, g).then_inc(s_pack, 1)
                pool.wait_ge(s_pack, n + 1)
                by_head(0, g).then_inc(s_qh, 1)
            reciprocal_deviations(2 * QT, TILES, 3)
            pool.wait_ge(s_bvo, 32)
            add_bias(0)
            for r in range(2):
                pool.memset(htail[r][:, :].bitcast(F32), 0.0).then_inc(s_psetup, 1)

            def qheads(b, slot, second):
                names, base = [t[0] for t in tasks_of(second, False)], tasks_before(b - 1, second)
                for g in range(G):
                    pool.wait_ge(s_read, base + names.index(f"QK{g}") + 1)
                    high_rows(g).then_inc(s_qkhi, 1)
                    if g == 0:
                        need(pool, s_sc, UNITS * (b - 1))
                    pool.wait_ge(s_qkhi, G * b + g + 1 - POOL_LESS)
                    packed(slot, g).then_inc(s_pack, 1)
                    pool.wait_ge(s_pack, G * b + g + 1 - POOL_LESS)
                    by_head(slot, g).then_inc(s_qh, 1)
                add_bias(b)
            qheads(1, 1, True)
            with pool.Fori(0, (B - 2) // 2) as i:
                qheads(2 * i + 2, 0, False)
                qheads(2 * i + 3, 1, False)
            pool.wait_ge(s_var2, 1)
            pool.tensor_tensor(rstd[:, 0:EARLY * GT], mv[:, 0:EARLY * GT, 1], expo[:, 0:EARLY * GT], ALU.pow).then_inc(s_rstd2, 1)
            pool.wait_ge(s_rstd2, 1)
            for k in range(EARLY):
                tiles = slice(GT * k, GT * (k + 1))
                pool.tensor_tensor(xn2[:, tiles, :], x1[:, tiles, :], mv[:, tiles, 0:1].to_broadcast([P, GT, P]),
                                   ALU.subtract).then_inc(s_centred, 1)
                pool.wait_ge(s_centred, k + 1)
                pool.tensor_tensor(xn2[:, tiles, :], xn2[:, tiles, :], rstd[:, tiles].unsqueeze(2).to_broadcast([P, GT, P]),
                                   ALU.mult).then_inc(s_xn2, 1)

            def split(raw, hi, lo, bias, count):
                w = hi.shape[-1]
                pool.tensor_tensor(hi[:, :], raw[:, 0:w], one[:, :].to_broadcast([P, w]), ALU.mult).then_inc(s_wh, 1)
                pool.tensor_copy(bias[:, :], raw[:, w:w + 2])
                pool.wait_ge(s_wh, count)
                pool.tensor_tensor(lo[:, :], raw[:, 0:w], hi[:, :].bitcast(F32), ALU.subtract).then_inc(s_w, 1)

            def add_shares(e, tiles=TT):
                for t in range(tiles):
                    pool.wait_ge(s_mix, TT * e + t + 1)
                    pool.tensor_tensor(acc[:, t, :], acc[:, t, :], mixed[t][:, :], ALU.add).then_inc(s_add, 1)

            def expert(e, first):
                def triple(c, head):
                    for r in range(WRING):
                        pool.wait_ge(s_raw[r], 16 * (FULL // WRING * e + (0 if head else c // WRING) + 1))
                        if not head:
                            pool.wait_ge(s_down, STEPS * e + TT * (c + r - WRING) + TT)
                        elif not first:
                            pool.wait_ge(s_down, STEPS * (e - 1) + TT * (FULL - WRING + r) + TT)
                        split(wraw[r], whi[r], wlo[r], wbias[r], CH * e + c + r + 1)
                    if head and first:
                        pool.wait_ge(s_var2, 2)
                        pool.tensor_tensor(rstd[:, EARLY * GT:TILES], mv[:, EARLY * GT:TILES, 1], expo[:, EARLY * GT:TILES],
                                           ALU.pow).then_inc(s_rstd2, 1)
                        pool.wait_ge(s_top2, TOP_LOGITS)
                        pool.tensor_tensor(second[:, :], euler[:, :], share[:, :], ALU.pow).then_inc(s_rexp, 1)
                    if head and not first:
                        add_shares(e - 1)
                triple(0, True)
                with pool.Fori(1, FULL // WRING) as i:
                    for r in range(WRING):
                        pool.wait_ge(s_raw[r], 16 * (FULL // WRING * e + i + 1))
                        pool.wait_ge(s_down, STEPS * e + TT * (WRING * i + r - WRING) + TT)
                        split(wraw[r], whi[r], wlo[r], wbias[r], CH * e + WRING * i + r + 1)
                pool.wait_ge(s_rawt, 16 * (e + 1))
                need(pool, s_down, STEPS * e)
                split(wtraw, wthi, wtlo, wtbias, CH * e + CH)
            experts(pool, expert)
            add_shares(E - 1, TT // 2)

        @block.scalar
        def _(act):
            def read_task(name, count, fb):
                if name == "TX":
                    act.wait_ge(s_task, count)
                    act.activation(xnT[:, :], misc[:, 0:S], ACT.Copy).then_inc(s_read, 1)
                elif name[:2] == "QK":
                    g = int(name[2])
                    act.wait_ge(s_task, count)
                    act.wait_ge(s_pack, G * fb + g - 1 - POOL_LESS)
                    for n in range(2):
                        ins = act.activation(qkf[g % 2][:, n, :], misc[:, n * S:(n + 1) * S], ACT.Identity,
                                             bias=bqk_sb[:, n, g:g + 1])
                    ins.then_inc(s_read, 1)
                elif name[:3] == "X1T":
                    act.wait_ge(s_task, count)
                    act.activation(acc[:, int(name[3]), :], misc[:, :], ACT.Copy).then_inc(s_read, 1)
                elif name[:2] == "XT":
                    act.wait_ge(s_task, count)
                    act.activation(xhi[int(name[2])], misc[:, :], ACT.Copy).then_inc(s_xhi, 1)

            def half1(m, parity):
                act.wait_ge(s_pt, 2 * m + 2)
                need(act, s_pv, m - 1)
                act.activation(probT[parity][:, 2:4, :, :], ptb[1][:, :], ACT.Copy).then_inc(s_pt1, 1)

            def exponentials(m, u, half):
                if half == 0:
                    act.wait_ge(s_top, m + 1)
                    need(act, s_pt, 2 * (m - 1))
                for j in (2 * half, 2 * half + 1):
                    ins = act.activation(prob[u % 2][:, j, :], masked[u % 2][:, j, :],
                                         ACT.Exp, bias=negtop[u % 4][:, j:j + 1], scale=-1.0)
                if half == 1:
                    ins.then_inc(s_exp, 1)

            def core(b, slot, k, first, last):
                order = tasks_of(first, last)
                base = tasks_before(b, first)

                def run(u, pos):
                    for n, (name, at, where) in enumerate(order):
                        if (at, where) == (u, pos):
                            read_task(name, base + n + 1, b + 1)
                for u in range(UNITS):
                    n = UNITS * b + u
                    if not (first and u == 0):
                        exponentials(n - 1, (u - 1) % UNITS, 0)
                    run(u, 0)
                    if not (first and u == 0):
                        exponentials(n - 1, (u - 1) % UNITS, 1)
                    if not (first and u < 2):
                        half1(n - 2, u % 2)
                    run(u, 1)
                    run(u, 2)

            act.wait_ge(s_psetup, 1)
            act.activation(first[:, :], expo[:, 0:1], ACT.Copy)
            act.wait_ge(s_w4, 16)
            for n in range(2):
                act.activation(wqk[:, n, :, :, :], w4[:, n, :].rearrange("p (g c) -> p g c", g=G).unsqueeze(2)
                               .to_broadcast([P, G, 4, 32]), ACT.Copy).then_inc(s_wqk, 1)
            act.wait_ge(s_front, 1)
            act.activation(xnT[:, :], misc[:, 0:S], ACT.Copy).then_inc(s_xnT0, 1)
            act.wait_ge(s_bqk, 16)
            for g in range(G):
                act.wait_ge(s_front, FRONT_TASKS.index(f"QK{g}") + 1)
                if g >= 2:
                    act.wait_ge(s_pack0 if g == 2 else s_pack, 1)
                for n in range(2):
                    ins = act.activation(qkf[g % 2][:, n, :], front_bank[g][:, n * S:(n + 1) * S], ACT.Identity,
                                         bias=bqk_sb[:, n, g:g + 1])
                ins.then_inc(s_front_read, 1)
            batches(act, core)
            exponentials(UNITS * B - 1, UNITS - 1, 0)
            exponentials(UNITS * B - 1, UNITS - 1, 1)
            half1(UNITS * B - 2, 0)
            half1(UNITS * B - 1, 1)
            base = tasks_before(B - 1, False) + len(LAST_TASKS)

            def finish(n):
                if n == 2:
                    act.wait_ge(s_x1t, 1)
                    act.activation(acc[:, TT - 1, :], misc[:, :], ACT.Copy).then_inc(s_add, TT)
                elif n == 3:
                    act.wait_ge(s_xt, 1)
                    act.activation(xhi[TT - 1], bank[5][:, :], ACT.Copy).then_inc(s_xhi, 1)

            def high(c, t, step):
                act.wait_ge(s_h, step + 1)
                need(act, s_down, step - 1)
                if c == FULL:
                    act.activation(htail[t % 2][0:TAIL, :], hid[t % 2][0:TAIL, :], ACT.Copy).then_inc(s_hhi, 1)
                else:
                    act.activation(hhi[t % 2][:, :], hid[t % 2][:, :], ACT.Copy).then_inc(s_hhi, 1)

            def step(c, bias, t, number, first, before):
                rows = TAIL if c == FULL else P
                act.wait_ge(s_gate, number + 1)
                act.activation(gact[t % 2][0:rows, :], bank[t % 2][0:rows, :], ACT.Silu,
                               bias=bias[0:rows, 0:1]).then_inc(s_silu, 1)
                if not first:
                    high(before, (t - 1) % TT, number - 1)

            def expert(e, head):
                def chunk(c, c_is, bias, first_chunk):
                    for t in range(TT):
                        if head and first_chunk:
                            finish(t)
                        step(c_is, bias, t, STEPS * e + TT * c + t, head and first_chunk and t == 0,
                             FULL if first_chunk and t == 0 else (c_is if t else 0))
                for r in range(WRING):
                    chunk(r, 0, wbias[r], r == 0)
                with act.Fori(1, FULL // WRING) as i:
                    for r in range(WRING):
                        chunk(WRING * i + r, 0, wbias[r], False)
                chunk(FULL, FULL, wtbias, False)
            experts(act, expert)
            high(FULL, TT - 1, STEPS * E - 1)

        @block.vector
        def _(dve):
            def statistics(tiles):
                for t in tiles:
                    ins = dve.bn_stats(stat[:, t, :], x1[:, t, :])
                ins.then_inc(s_stat, 1)

            def variances(t0, t1, count):
                dve.wait_ge(s_stat, count - 1)
                for t in range(t0, t1):
                    ins = dve.bn_aggr(mv[:, t, :], stat[:, t, :])
                ins.then_inc(s_stat, 1)
                dve.wait_ge(s_stat, count)
                dve.tensor_scalar(mv[:, t0:t1, 1], mv[:, t0:t1, 1], EPS, None, ALU.add).then_inc(s_var, 1)

            def normalise(b):
                dve.wait_ge(s_rstd, b + 1 if isinstance(b, int) and b < 2 else 3)
                for qt in range(QT):
                    t = QT * b + qt
                    ins = dve.tensor_scalar(xn[:, qt, :], x1[:, bass.ds(t, 1), :], mv[:, bass.ds(t, 1), 0],
                                            rstd[:, bass.ds(t, 1)], ALU.subtract, ALU.mult)
                ins.then_inc(s_xn, 1)

            def bias_mask(b, slot, k):
                dve.wait_ge(s_mask[slot], 16 * (k + 1))
                need(dve, s_sc, UNITS * (b - 1))
                dve.tensor_scalar(maskb[slot][:, :, :], mask_sb[slot][:, :, :], 0.0, NEG, ALU.is_equal, ALU.mult).then_inc(s_mb, 1)

            def values(slot, source):
                return dve.tensor_tensor(vaug[slot][:, :, :, 0:DK],
                                         source[:, 0:S].rearrange("p (t h d) -> p t h d", t=QT, d=DK),
                                         bv_sb[:, :].rearrange("p (h d) -> p h d", d=DK).unsqueeze(1)
                                         .to_broadcast([P, QT, HEADS, DK]), ALU.add)

            def read_task(name, count, fb, fslot, bb):
                if name == "V":
                    dve.wait_ge(s_task, count)
                    need(dve, s_pv, UNITS * (fb - 1))
                    values(fslot, misc).then_inc(s_read, 1)
                elif name[:3] == "OVT":
                    qt = int(name[3])
                    tile = QT * (bb + 1 if qt == 0 else bb) + qt
                    dve.wait_ge(s_task, count)
                    o = misc[:, :].rearrange("p (h r) -> p h r", r=32)
                    dve.reciprocal(rden[:, :], o[:, :, DK]).then_inc(s_rden, 1)
                    dve.wait_ge(s_rden, tile + 1)
                    dve.tensor_tensor(onat[:, qt, :].rearrange("p (h d) -> p h d", d=DK), o[:, :, 0:DK],
                                      rden[:, :].unsqueeze(2).to_broadcast([P, HEADS, DK]),
                                      ALU.mult).then_inc(s_read, 1)
                elif name[:2] == "XT":
                    k = int(name[2])
                    dve.wait_ge(s_xhi, k + 1)
                    dve.tensor_tensor(xlo[k], misc[:, :], xhi[k].bitcast(F32), ALU.subtract).then_inc(s_read, 1)
                elif name == "OT":
                    dve.wait_ge(s_task, count)
                    dve.tensor_copy(oT[:, :], misc[:, 0:S]).then_inc(s_read, 1)
                elif name == "WO":
                    dve.wait_ge(s_task, count)
                    dve.wait_ge(s_xb, bb + 1)
                    tiles = bass.ds(QT * bb, QT)
                    dve.tensor_tensor(x1[:, tiles, :], misc[:, 0:S].rearrange("p (t c) -> p t c", t=QT),
                                      x1[:, tiles, :], ALU.add).then_inc(s_read, 1)
                    dve.wait_ge(s_read, count)
                    for qt in range(QT):
                        ins = dve.bn_stats(stat[:, bass.ds(QT * bb + qt, 1), :], x1[:, bass.ds(QT * bb + qt, 1), :])
                    ins.then_inc(s_stat2, 1)

            def copy_ov(count, transposed):
                dve.wait_ge(s_pv, count)
                need(dve, s_task, transposed)
                dve.tensor_copy(ov[:, :, :], ovb[:, :]).then_inc(s_ov, 1)

            def variances2(t0, t1, batches_made):
                dve.wait_ge(s_stat2, batches_made)
                for t in range(t0, t1):
                    ins = dve.bn_aggr(mv[:, t, :], stat[:, t, :])
                ins.then_inc(s_aggr2, 1)
                dve.wait_ge(s_aggr2, 1 if t0 == 0 else 2)
                dve.tensor_scalar(mv[:, t0:t1, 1], mv[:, t0:t1, 1], EPS, None, ALU.add).then_inc(s_var2, 1)

            def core(b, slot, k, first, last):
                order = tasks_of(first, last)
                base = tasks_before(b, first)

                def run(u, pos):
                    for n, (name, at, where) in enumerate(order[:-1]):
                        if (at, where) == (u, pos):
                            read_task(name, base + n + 1, b + 1, 1 - slot, b - 1)
                for u in range(UNITS):
                    n = UNITS * b + u
                    qt = u // G
                    if u == 0 and not last:
                        normalise(b + 1)
                    dve.wait_ge(s_sc, n + 1)
                    need(dve, s_exp, n - 1)
                    if u == 0:
                        dve.wait_ge(s_mb, b + 1)
                    dve.memset(turn[:, u:u + 1], 0.0)
                    for j in range(HG):
                        ins = dve.tensor_tensor_reduce(
                            out=masked[u % 2][:, j, :], in0=scores[u % 2][j // 2][:, (j % 2) * S:(j % 2 + 1) * S],
                            in1=maskb[slot][:, qt, :], scale=-SCALE, scalar=NO_KEY, op0=ALU.add, op1=ALU.min,
                            accum_out=negtop[u % 4][:, j:j + 1])
                    ins.then_inc(s_top, 1)
                    run(u, 0)
                    if u == 0 and not first:
                        read_task("OVT0", base, 0, 0, b - 2)
                    if not (first and u < 2):
                        half0(n - 2, u % 2)
                    run(u, 1)
                    if u == 6:
                        copy_ov(UNITS * b + G, 0 if first else base + 1 + [t[0] for t in order].index("OVT1"))
                    if u == 2 and not first:
                        copy_ov(UNITS * b, base)
                    if first and u == 2:
                        variances(2 * QT, TILES, 6)
                    if last and u == 0:
                        variances2(0, EARLY * GT, B - QT)
                    if last and u == 1:
                        dve.wait_ge(s_ffnc, 32)
                        dve.tensor_copy(rsplit[:, 0, :], rw[:, :]).then_inc(s_rsplit, 1)
                        dve.wait_ge(s_rsplit, 1)
                        dve.tensor_tensor(rsplit[:, 1, :], rw[:, :], rsplit[:, 0, :].bitcast(F32), ALU.subtract).then_inc(s_rsplit, 1)
                    if u == 4 and not last:
                        bias_mask(b + 1, 1 - slot, k if slot == 0 else k + 1)
                    run(u, 2)

            def half0(m, parity):
                dve.wait_ge(s_pt, 2 * m + 1)
                need(dve, s_pv, m - 1)
                dve.tensor_copy(probT[parity][:, 0:2, :, :], ptb[0][:, :]).then_inc(s_pt0, 1)

            dve.wait_ge(s_x0, 16)
            statistics(range(QT))
            variances(0, QT, 2)
            dve.wait_ge(s_xsecond, 16)
            statistics(range(QT, 2 * QT))
            variances(QT, 2 * QT, 4)
            normalise(0)
            dve.wait_ge(s_x, 16)
            statistics(range(2 * QT, TILES))
            bias_mask(0, 0, 0)
            dve.wait_ge(s_cst, 16)
            high_rows, packed, by_head = grouped(dve)
            for n, g in enumerate((0, 2)):
                dve.wait_ge(s_front_read, g + 1)
                high_rows(g).then_inc(s_qkhi0, 1)
                dve.wait_ge(s_qkhi0, n + 1)
                packed(0, g).then_inc(s_pack0, 1)
                dve.wait_ge(s_pack0, n + 1)
                by_head(0, g).then_inc(s_qh0, 1)
            dve.wait_ge(s_front, FRONT_TASKS.index("V") + 1)
            dve.wait_ge(s_psetup, 3)
            dve.wait_ge(s_bvo, 32)
            values(0, front_v).then_inc(s_v0, 1)
            dve.wait_ge(s_psetup, 6)
            batches(dve, core)
            half0(UNITS * B - 2, 0)
            half0(UNITS * B - 1, 1)
            base = tasks_before(B - 1, False) + len(LAST_TASKS)
            read_task("OVT0", base, 0, 0, B - 2)
            copy_ov(UNITS * B, base)

            def finish(n):
                if n == 0:
                    read_task("OVT1", base + 1, 0, 0, B - 1)
                elif n == 1:
                    read_task("OT", base + 2, 0, 0, B - 1)
                    read_task("WO", base + 3, 0, 0, B - 1)
                    variances2(EARLY * GT, TILES, B)
                elif n == 2:
                    dve.wait_ge(s_rstd2, 2)
                    for t in range(EARLY * GT, TILES):
                        ins = dve.tensor_scalar(xn2[:, t, :], x1[:, t, :], mv[:, t, 0:1], rstd[:, t:t + 1],
                                                ALU.subtract, ALU.mult)
                    ins.then_inc(s_xn2, 1)
                elif n == 3:
                    dve.wait_ge(s_xhi, TT)
                    dve.tensor_tensor(xlo[TT - 1], bank[5][:, :], xhi[TT - 1].bitcast(F32), ALU.subtract).then_inc(s_xlo, 1)
                    dve.wait_ge(s_psetup, 8)
                    dve.wait_ge(s_ffnc, 32)

            other = lg[:, :, :].unsqueeze(2).to_broadcast([P, TILES, E, E])
            own = lg[:, :, :].unsqueeze(3).to_broadcast([P, TILES, E, E])
            before = cst[:, C_GE:C_GE + E * E].rearrange("p (e f) -> p e f", f=E).unsqueeze(1).to_broadcast([P, TILES, E, E])
            after = cst[:, C_GT:C_GT + E * E].rearrange("p (e f) -> p e f", f=E).unsqueeze(1).to_broadcast([P, TILES, E, E])

            def top_two(n):
                if n == 4:
                    dve.wait_ge(s_rt, 1)
                    logits = bank[6][:, 0:TILES * 2 * E].rearrange("p (t h e) -> p t e h", h=2, e=E)
                    dve.tensor_reduce(lg[:, :, :], logits, AX.X, ALU.add).then_inc(s_top2, 1)
                elif n == 5:
                    dve.wait_ge(s_top2, 1)
                    dve.tensor_tensor(cge[:, :, :, :], other, own, ALU.is_ge).then_inc(s_top2, 1)
                    dve.tensor_tensor(cgt[:, :, :, :], other, own, ALU.is_gt).then_inc(s_top2, 1)
                elif n == 6:
                    dve.wait_ge(s_top2, 3)
                    dve.tensor_reduce(ltop[:, :], lg[:, :, :], AX.X, ALU.max).then_inc(s_top2, 1)
                    dve.tensor_tensor(cge[:, :, :, :], cge[:, :, :, :], before, ALU.mult).then_inc(s_top2, 1)
                    dve.tensor_tensor(cgt[:, :, :, :], cgt[:, :, :, :], after, ALU.mult).then_inc(s_top2, 1)
                elif n == 7:
                    dve.wait_ge(s_top2, 6)
                    dve.tensor_tensor(cge[:, :, :, :], cge[:, :, :, :], cgt[:, :, :, :], ALU.add).then_inc(s_top2, 1)
                    dve.wait_ge(s_top2, 7)
                    dve.tensor_reduce(rank[:, :, :], cge[:, :, :, :], AX.X, ALU.add).then_inc(s_top2, 1)
                elif n == 8:
                    dve.wait_ge(s_top2, 8)
                    dve.scalar_tensor_tensor(out=lg[:, :, :], in0=rank[:, :, :], scalar=1.5, in1=lg[:, :, :],
                                             op0=ALU.is_lt, op1=ALU.mult).then_inc(s_top2, 1)
                    dve.wait_ge(s_top2, 9)
                    dve.tensor_reduce(wsum[:, :], lg[:, :, :], AX.X, ALU.add).then_inc(s_top2, 1)
                    dve.wait_ge(s_top2, 10)
                    dve.scalar_tensor_tensor(out=share[:, :], in0=ltop[:, :], scalar=-2.0, in1=wsum[:, :],
                                             op0=ALU.mult, op1=ALU.add).then_inc(s_top2, 1)
                elif n == 10:
                    dve.wait_ge(s_rexp, 1)
                    dve.scalar_tensor_tensor(out=wexp[:, :, :], in0=rank[:, :, :], scalar=0.5,
                                             in1=second[:, :].unsqueeze(2).to_broadcast([P, TILES, E]),
                                             op0=ALU.is_lt, op1=ALU.max).then_inc(s_top2, 1)
                    dve.tensor_scalar(wsum[:, :], second[:, :], 1.0, None, ALU.add).then_inc(s_top2, 1)
                    dve.wait_ge(s_top2, 13)
                    dve.reciprocal(share[:, :], wsum[:, :]).then_inc(s_top2, 1)
                    dve.scalar_tensor_tensor(out=rank[:, :, :], in0=rank[:, :, :], scalar=1.5, in1=wexp[:, :, :],
                                             op0=ALU.is_lt, op1=ALU.mult).then_inc(s_top2, 1)
                    dve.wait_ge(s_top2, 15)
                    dve.tensor_tensor(mixw[:, :, :].rearrange("p e t -> p t e"), rank[:, :, :],
                                      share[:, :].unsqueeze(2).to_broadcast([P, TILES, E]), ALU.mult).then_inc(s_top2, 1)
                elif n == 11:
                    dve.wait_ge(s_wT, 1)
                    dve.tensor_copy(mixwT[:, :], bank[3][0:E * TILES, 0:P]).then_inc(s_wTc, 1)

            def low(c, t, step):
                dve.wait_ge(s_hhi, step + 1)
                if c == FULL:
                    dve.tensor_tensor(htail[t % 2][UP0:UP0 + TAIL, :], hid[t % 2][0:TAIL, :],
                                      htail[t % 2][0:TAIL, :].bitcast(F32), ALU.subtract).then_inc(s_hlo, 1)
                else:
                    dve.tensor_tensor(hlo[t % 2][:, :], hid[t % 2][:, :], hhi[t % 2][:, :].bitcast(F32),
                                      ALU.subtract).then_inc(s_hlo, 1)

            def mix(e, t):
                dve.wait_ge(s_down, STEPS * e + TT * FULL + t + 1)
                if t == 0:
                    dve.wait_ge(s_mixb, 16)
                dve.wait_ge(s_add, TT * e + t + 1)
                dve.scalar_tensor_tensor(out=mixed[t][:, :], in0=bank[4 + t][:, :], scalar=db_sb[:, bass.ds(e, 1)],
                                         in1=mixb[:, bass.ds(e * TOK + t * TN, TN)], op0=ALU.add,
                                         op1=ALU.mult).then_inc(s_mix, 1)

            def step(c_is, bias, t, number, ups, first, before):
                need(dve, s_hlo, number - 1)
                dve.wait_ge(s_silu, number + 1)
                if c_is == FULL:
                    dve.scalar_tensor_tensor(out=hid[t % 2][0:TAIL, :], in0=bank[t % 2][UP0:UP0 + TAIL, :],
                                             scalar=bias[UP0:UP0 + TAIL, 1:2],
                                             in1=gact[t % 2][0:TAIL, :], op0=ALU.add, op1=ALU.mult).then_inc(s_h, 1)
                else:
                    dve.wait_ge(s_up, ups)
                    dve.scalar_tensor_tensor(out=hid[t % 2][:, :], in0=bank[2 + t % 2][:, :],
                                             scalar=bias[:, 1:2], in1=gact[t % 2][:, :],
                                             op0=ALU.add, op1=ALU.mult).then_inc(s_h, 1)
                if not first:
                    low(before, (t - 1) % TT, number - 1)

            def expert(e, head):
                def chunk(c, c_is, bias, first_chunk):
                    for t in range(TT):
                        if head and c_is == 0 and isinstance(c, int):
                            finish(TT * c + t)
                            top_two(TT * c + t)
                        step(c_is, bias, t, STEPS * e + TT * c + t, (STEPS - TT) * e + TT * c + t + 1, head and first_chunk and t == 0,
                             FULL if first_chunk and t == 0 else (c_is if t else 0))
                        if first_chunk and not head:
                            mix(e - 1, t)
                for r in range(WRING):
                    chunk(r, 0, wbias[r], r == 0)
                with dve.Fori(1, FULL // WRING) as i:
                    for r in range(WRING):
                        chunk(WRING * i + r, 0, wbias[r], False)
                chunk(FULL, FULL, wtbias, False)
            experts(dve, expert)
            low(FULL, TT - 1, STEPS * E - 1)
            for t in range(TT):
                mix(E - 1, t)
                if t >= TT // 2:
                    dve.wait_ge(s_mix, TT * (E - 1) + t + 1)
                    dve.tensor_tensor(acc[:, t, :], acc[:, t, :], mixed[t][:, :], ALU.add).then_inc(s_addlast, 1)

        @block.tensor
        def _(pe):
            def run_task(name, count, fb, fslot, fk, bb):
                need(pe, s_read, count - 1)
                if name == "TX":
                    pe.wait_ge(s_xn, fb + 1)
                    for qt in range(QT):
                        ins = pe.transpose(misc[:, qt * P:(qt + 1) * P], xn[:, qt, :], ident)
                    ins.then_inc(s_task, 1)
                elif name[:2] == "QK":
                    g = int(name[2])
                    pe.wait_ge(s_ctx[fslot], 16 * (fk + 1))
                    for n, moving in ((0, xnT), (1, ctx_sb[fslot])):
                        ins = pe.matmul(misc[:, n * S:(n + 1) * S], wqk[:, n, g, :, :].rearrange("p q c -> p (q c)"), moving[:, :], start=True, stop=True)
                    ins.then_inc(s_task, 1)
                elif name == "V":
                    for kt in range(QT):
                        ins = pe.matmul(misc[:, kt * P:(kt + 1) * P], ctx_sb[fslot][:, kt * P:(kt + 1) * P], w4[:, 2, :],
                                        start=True, stop=True)
                    ins.then_inc(s_task, 1)
                elif name[:3] == "OVT":
                    qt = int(name[3])
                    pe.wait_ge(s_ov, QT * (bb + 1 if qt == 0 else bb) + qt + 1)
                    for g in range(G):
                        ins = pe.transpose(misc[:, g * P:(g + 1) * P], ov[:, g, :], ident)
                    ins.then_inc(s_task, 1)
                elif name == "OT":
                    for qt in range(QT):
                        ins = pe.transpose(misc[:, qt * P:(qt + 1) * P], onat[:, qt, :], ident)
                    ins.then_inc(s_task, 1)
                elif name[:3] == "X1T":
                    for n in range(GT):
                        ins = pe.transpose(misc[:, n * P:(n + 1) * P], x1[:, GT * int(name[3]) + n, :], ident)
                    ins.then_inc(s_task, 1)
                elif name[:2] == "XT":
                    pe.wait_ge(s_xn2, int(name[2]) + 1)
                    for n in range(GT):
                        ins = pe.transpose(misc[:, n * P:(n + 1) * P], xn2[:, GT * int(name[2]) + n, :], ident)
                    ins.then_inc(s_task, 1)
                elif name == "WO":
                    for qt in range(QT):
                        ins = pe.matmul(misc[:, qt * P:(qt + 1) * P], oT[:, qt * P:(qt + 1) * P], w4[:, 3, :],
                                        start=True, stop=True)
                    ins.then_inc(s_task, 1)

            def score(b, slot, u, first):
                n = UNITS * b + u
                qt, g = u // G, u % G
                if qt == 0:
                    if first:
                        pe.wait_ge(s_qh if g % 2 else s_qh0, g // 2 + 1)
                    else:
                        pe.wait_ge(s_qh, G * b + g + 1 - POOL_LESS)
                need(pe, s_top, n - 1)
                for j in range(HG):
                    ins = pe.matmul(scores[u % 2][j // 2][:, (j % 2) * S:(j % 2 + 1) * S],
                                    qhead[slot][:, g, j, qt * P:(qt + 1) * P], qkpack[slot][:, g, 1, :],
                                    start=True, stop=True)
                ins.then_inc(s_sc, 1)

            def transpose_probs(m, parity):
                pe.wait_ge(s_exp, m + 1)
                for half, copied in ((0, s_pt0), (1, s_pt1)):
                    need(pe, copied, m)
                    for j in range(2):
                        for kt in range(QT):
                            ins = pe.transpose(ptb[half][:, (2 * j + kt) * P:(2 * j + kt + 1) * P],
                                               prob[parity][:, 2 * half + j, kt * P:(kt + 1) * P], ident)
                    ins.then_inc(s_pt, 1)

            def weigh_values(m, slot, u, tiles):
                g = u % G
                pe.wait_ge(s_pt0, m + 1)
                pe.wait_ge(s_pt1, m + 1)
                if g == 0:
                    need(pe, s_ov, tiles)
                for kt in range(QT):
                    for j in range(HG):
                        ins = pe.matmul(ovb[32 * j:32 * j + 32, g * P:(g + 1) * P], vaug[slot][:, kt, HG * g + j, :],
                                        probT[u % 2][:, j, kt, :], start=kt == 0, stop=kt == QT - 1)
                ins.then_inc(s_pv, 1)

            def core(b, slot, k, first, last):
                order = tasks_of(first, last)
                base = tasks_before(b, first)
                fk = k if slot == 0 else k + 1

                def run(u, pos):
                    for n, (name, at, where) in enumerate(order):
                        if (at, where) == (u, pos):
                            run_task(name, base + n + 1, b + 1, 1 - slot, fk, b - 1)
                for u in range(UNITS):
                    n = UNITS * b + u
                    if first and u == 1:
                        pe.wait_ge(s_v0, 1)
                    score(b, slot, u, first)
                    run(u, 0)
                    if not (first and u < 2):
                        transpose_probs(n - 2, u % 2)
                    run(u, 1)
                    if u == 3 and not first:
                        pe.wait_ge(s_read, base)
                    if not (first and u < 3):
                        weigh_values(n - 3, slot if u >= 3 else 1 - slot, (u - 3) % UNITS,
                                     QT * b + (u - 3) // G)
                    run(u, 2)

            def project(n, g, moving):
                return pe.matmul(front_bank[g][:, n * S:(n + 1) * S], wqk[:, n, g, :, :].rearrange("p q c -> p (q c)"),
                                 moving[:, :], start=True, stop=True)

            pe.wait_ge(s_wqk, 2)
            pe.wait_ge(s_ctx[0], 16)
            project(1, 0, ctx_sb[0])
            pe.wait_ge(s_cst, 16)
            pe.wait_ge(s_xn, 1)
            for qt in range(QT):
                ins = pe.transpose(misc[:, qt * P:(qt + 1) * P], xn[:, qt, :], ident)
            ins.then_inc(s_front, 1)
            project(1, 1, ctx_sb[0])
            pe.wait_ge(s_xnT0, 1)
            project(0, 0, xnT).then_inc(s_front, 1)
            project(0, 1, xnT).then_inc(s_front, 1)
            for kt in range(QT):
                ins = pe.matmul(front_v[:, kt * P:(kt + 1) * P], ctx_sb[0][:, kt * P:(kt + 1) * P], w4[:, 2, :],
                                start=True, stop=True)
            ins.then_inc(s_front, 1)
            for g in (2, 3):
                project(1, g, ctx_sb[0])
                project(0, g, xnT).then_inc(s_front, 1)
            batches(pe, core)
            last = UNITS * B
            transpose_probs(last - 2, 0)
            weigh_values(last - 3, 1, UNITS - 3, 0)
            transpose_probs(last - 1, 1)
            weigh_values(last - 2, 1, UNITS - 2, 0)
            weigh_values(last - 1, 1, UNITS - 1, 0)
            base = tasks_before(B - 1, False) + len(LAST_TASKS)
            pe.wait_ge(s_read, base)

            def last_transposes(dst, source):
                for n in range(GT):
                    ins = pe.transpose(dst[:, n * P:(n + 1) * P], source[:, EARLY * GT + n, :], ident)
                return ins

            def route(tiles):
                for t in tiles:
                    dst, part = bank[6][:, 2 * E * t:2 * E * (t + 1)], slice(t % GT * P, (t % GT + 1) * P)
                    pe.matmul(dst, xhi[t // GT][:, part], rsplit[:, :, :].rearrange("p h e -> p (h e)"), start=True, stop=False)
                    ins = pe.matmul(dst, xlo[t // GT][:, part], rsplit[:, :, :].rearrange("p h e -> p (h e)"), start=False, stop=True)
                return ins

            def finish(n, up):
                if (n, up) == (0, 1):
                    run_task("OVT1", base + 1, 0, 0, 0, B - 1)
                elif (n, up) == (1, 0):
                    run_task("OT", base + 2, 0, 0, 0, B - 1)
                elif (n, up) == (1, 1):
                    run_task("WO", base + 3, 0, 0, 0, B - 1)
                elif (n, up) == (2, 0):
                    pe.wait_ge(s_rsplit, 2)
                    route(range(EARLY * GT // 2))
                elif (n, up) == (2, 1):
                    pe.wait_ge(s_read, base + 3)
                    last_transposes(misc, x1).then_inc(s_x1t, 1)
                elif (n, up) == (3, 0):
                    route(range(EARLY * GT // 2, EARLY * GT * 3 // 4))
                    pe.wait_ge(s_xn2, TT)
                    last_transposes(bank[5], xn2).then_inc(s_xt, 1)
                    route(range(EARLY * GT * 3 // 4, EARLY * GT))
                    pe.wait_ge(s_xlo, 1)
                    route(range(EARLY * GT, TILES)).then_inc(s_rt, 1)
                elif (n, up) == (4, 1):
                    pe.wait_ge(s_top2, 1)
                elif (n, up) == (5, 0):
                    pe.wait_ge(s_add, TT)
                elif (n, up) == (11, 0):
                    pe.wait_ge(s_top2, TOP_WEIGHTS)
                    pe.wait_ge(s_h, 10)
                    pe.transpose(bank[3][0:E * TILES, 0:P], mixw[:, :, :], ident).then_inc(s_wT, 1)
                elif (n, up) == (11, 1):
                    pe.wait_ge(s_wTc, 1)

            def up_products(dst, hi, lo, t):
                pe.matmul(dst, hi, xhi[t], start=True, stop=False)
                pe.matmul(dst, hi, xlo[t], start=False, stop=False)
                return pe.matmul(dst, lo, xhi[t], start=False, stop=True)

            def down(c_is, r, t, number, start, mixed_before):
                pe.wait_ge(s_hlo, number + 1)
                if start:
                    need(pe, s_mix, mixed_before)
                dst = bank[4 + t][:, :]
                if c_is == FULL:
                    pe.matmul(dst, wthi[:, P:2 * P], htail[t % 2][:, :], start=False, stop=False)
                    pe.matmul(dst, wtlo[:, P:2 * P], htail[t % 2][:, :], start=False, stop=True).then_inc(s_down, 1)
                else:
                    hi, lo = whi[r][:, 2 * P:3 * P], wlo[r][:, 2 * P:3 * P]
                    pe.matmul(dst, hi, hhi[t % 2][:, :], start=start, stop=False)
                    pe.matmul(dst, hi, hlo[t % 2][:, :], start=False, stop=False)
                    pe.matmul(dst, lo, hhi[t % 2][:, :], start=False, stop=False).then_inc(s_down, 1)

            def expert(e, head):
                def chunk(c, c_is, r, kind):
                    for t in range(TT):
                        number = STEPS * e + TT * c + t
                        if t == 0:
                            pe.wait_ge(s_w, CH * e + c + 1)
                        need(pe, s_silu, number - 1)
                        if c_is == FULL or kind == 0 and t < 2 and not head:
                            pe.wait_ge(s_h, number - 1)
                        if head and kind < WRING and isinstance(c, int) and c_is == 0:
                            finish(number, 0)
                        if c_is == FULL:
                            up_products(bank[t % 2][:, :], wthi[:, 0:P], wtlo[:, 0:P], t).then_inc(s_gate, 1)
                        else:
                            up_products(bank[t % 2][:, :], whi[r][:, 0:P], wlo[r][:, 0:P], t).then_inc(s_gate, 1)
                            need(pe, s_h, number - 1)
                            if head and kind < WRING and isinstance(c, int):
                                finish(number, 1)
                            up_products(bank[2 + t % 2][:, :], whi[r][:, P:2 * P], wlo[r][:, P:2 * P], t).then_inc(s_up, 1)
                        td = (t - LAG) % TT
                        if t >= LAG:
                            down(c_is, r, td, number - LAG, kind == 0, 0 if head else TT * (e - 1) + td + 1)
                        elif kind == 0:
                            if not head:
                                down(FULL, 0, td, number - LAG, False, 0)
                        else:
                            down(0, (r - 1) % WRING, td, number - LAG, kind == 1, 0 if head else TT * (e - 1) + td + 1)
                for r in range(WRING):
                    chunk(r, 0, r, r)
                with pe.Fori(1, FULL // WRING) as i:
                    for r in range(WRING):
                        chunk(WRING * i + r, 0, r, 2)
                chunk(FULL, FULL, 0, 2)
            experts(pe, expert)
            for t in range(TT - LAG, TT):
                down(FULL, 0, t, STEPS * (E - 1) + TT * FULL + t, False, 0)


def kernel(x, ctx_1024, mask_BxSxS2_ik0, L0_xattn_wq, L0_xattn_bq, L0_xattn_wk, L0_xattn_bk, L0_xattn_wv,
           L0_xattn_bv, L0_xattn_wo, L0_xattn_bo, L0_ffn_gate_w, L0_ffn_gate_b, L0_ffn_up_w, L0_ffn_up_b,
           L0_ffn_down_w, L0_ffn_down_b, L0_ffn_router_w):
    import numpy as np
    import concourse.bacc as bacc
    from concourse.bass_utils import run_bass_kernel_spmd

    a = lambda v: np.asarray(v)
    x, ctxv, mask = a(x), a(ctx_1024), a(mask_BxSxS2_ik0)
    gw, uw, dw = a(L0_ffn_gate_w), a(L0_ffn_up_w), a(L0_ffn_down_w)
    gb, ub = a(L0_ffn_gate_b), a(L0_ffn_up_b)
    cut = FULL * P

    consts = np.zeros((P, C_N), np.float32)
    consts[:, C_ID:C_ID + P] = np.eye(P)
    row = np.arange(P)
    consts[:, C_LOQ] = (row // 32) % 2
    consts[:, C_LOK] = row // 64
    for j in range(HG):
        consts[:, C_HEAD + j] = (row % 32) // DK == j
    earlier = np.tril(np.ones((E, E)), -1)
    consts[:, C_GE:C_GE + E * E] = earlier.reshape(1, -1)
    consts[:, C_GT:C_GT + E * E] = earlier.T.reshape(1, -1)

    wts = np.stack([a(w).T for w in (L0_xattn_wq, L0_xattn_wk, L0_xattn_wv, L0_xattn_wo)], 1)
    bqk = np.stack([np.concatenate([a(b).reshape(G, 32).T] * 4) for b in (L0_xattn_bq, L0_xattn_bk)], 1)
    gate = gw[:, :, :cut].reshape(E, P, FULL, P).transpose(0, 2, 1, 3)
    up = uw[:, :, :cut].reshape(E, P, FULL, P).transpose(0, 2, 1, 3)
    dn = dw[:, :cut].reshape(E, FULL, P, P)
    biases = [b[:, :cut].reshape(E, FULL, P, 1) for b in (gb, ub)]
    wfull = np.concatenate([gate, up, dn] + biases, 3).reshape(E * FULL * P, 3 * P + 2)
    wtail = np.zeros((E, P, 2 * P + 2), np.float32)
    wtail[:, :, 0:TAIL] = gw[:, :, cut:]
    wtail[:, :, UP0:UP0 + TAIL] = uw[:, :, cut:]
    wtail[:, 0:TAIL, P:2 * P] = dw[:, cut:]
    wtail[:, UP0:UP0 + TAIL, P:2 * P] = dw[:, cut:]
    wtail[:, 0:TAIL, 2 * P] = gb[:, cut:]
    wtail[:, UP0:UP0 + TAIL, 2 * P + 1] = ub[:, cut:]

    arrays = {
        "x": x.reshape(TOK, D),
        "ctxT": ctxv.reshape(TOK, D).T,
        "mask": mask.reshape(TOK, S),
        "wts": wts, "bqk": bqk, "bv": a(L0_xattn_bv), "bo": a(L0_xattn_bo), "consts": consts,
        "wfull": wfull, "wtail": wtail.reshape(E * P, 2 * P + 2),
        "dbT": a(L0_ffn_down_b).T, "router": a(L0_ffn_router_w),
    }
    nc = bacc.Bacc("TRN2", target_bir_lowering=False, num_devices=1)
    fed, args = {}, []
    for name, v in arrays.items():
        v = np.ascontiguousarray(v)
        fed[f"in_{name}"] = v
        args.append(nc.dram_tensor(f"in_{name}", v.shape, mybir.dt.from_np(v.dtype), kind="ExternalInput").ap())
    args.append(nc.dram_tensor("mixw_scratch", (E * TOK,), F32, kind="Internal").ap())
    args.append(nc.dram_tensor("outT", (P, TOK), F32, kind="ExternalOutput").ap())
    program(nc, *args)
    r = run_bass_kernel_spmd(nc, [fed], core_ids=[0])
    return r.results[0]["outT"].T.reshape(B, S, D)
```
